# Optimizing a Trainium2 kernel written in Bass

```python
import numpy as np
import jax
import jax.numpy as jnp

def _softmax(x, axis=-1):
    return jax.nn.softmax(x, axis=axis)

def _gelu(x):
    return jax.nn.gelu(x, approximate=True)

def _silu(x):
    return jax.nn.silu(x)

def _sigmoid(x):
    return jax.nn.sigmoid(x)

def _layernorm(x, axis=-1, eps=1e-05):
    m = jnp.mean(x, axis=axis, keepdims=True)
    v = jnp.var(x, axis=axis, keepdims=True)
    return (x - m) / jnp.sqrt(v + eps)

def _scatter_add(tgt, idx, src, axis=0):
    return tgt.at[idx].add(src)

def _segment_sum(src, seg, n):
    return jax.ops.segment_sum(src, seg, n)
kernel_name = 'mk_audio_tower_d1_tok_audfeat768_r4_e3d01b'

def setup_inputs(seed: int=0):
    np.random.seed(seed)
    _w = jnp.asarray

    def _rec_inputs():
        import jax
        import jax.numpy as jnp
        _rk = jax.random.key(seed)
        x = -0.000253961 + 1 * jax.random.normal(jax.random.fold_in(_rk, 1), (128, 90, 750), jnp.float32)
        return x
    x = _rec_inputs()

    def _L0_tok_setup():
        import jax, jax.numpy as jnp
        import numpy as np
        CHANNELS = 90
        PATCH = 16
        EMBED = 192
        key = jax.random.key(seed)
        k_x, k_w, k_b = jax.random.split(key, 3)
        in_feat = CHANNELS * PATCH
        x = jax.random.normal(k_x, (128, CHANNELS, 512), dtype=jnp.float32)
        bound = 1.0 / np.sqrt(in_feat)
        W = jax.random.uniform(k_w, (EMBED, in_feat), dtype=jnp.float32, minval=-bound, maxval=bound)
        b = jax.random.uniform(k_b, (EMBED,), dtype=jnp.float32, minval=-bound, maxval=bound)
        return {'x': x, 'W': W, 'b': b}
    _L0_tok_all = _L0_tok_setup()
    _L0_tok_in = {k: v for k, v in _L0_tok_all.items() if k in ('W', 'b')}
    del _L0_tok_all

    def _L0_attn_setup():
        import jax, jax.numpy as jnp
        import numpy as np
        B, S, D, H = (8, 512, 192, 192)
        key = jax.random.key(seed)
        kx, kq, kk, kv = jax.random.split(key, 4)
        scale = 1.0 / np.sqrt(D)
        return {'x': jax.random.normal(kx, (B, S, D), dtype=jnp.float32), 'Wq': jax.random.normal(kq, (D, H), dtype=jnp.float32) * scale, 'Wk': jax.random.normal(kk, (D, H), dtype=jnp.float32) * scale, 'Wv': jax.random.normal(kv, (D, H), dtype=jnp.float32) * scale}
    _L0_attn_all = _L0_attn_setup()
    _L0_attn_in = {k: v for k, v in _L0_attn_all.items() if k in ('Wq', 'Wk', 'Wv')}
    del _L0_attn_all

    def _L0_ffn_setup():
        import jax, jax.numpy as jnp
        import numpy as np
        B_SZ, S, D = (8, 128, 192)
        H = 12
        N_EXP = 8
        RANK = 16
        ALPHA = 32
        TOP_K = 2
        key = jax.random.key(seed)
        ks = jax.random.split(key, 9)
        x = jax.random.normal(ks[0], (B_SZ, S, D), jnp.float32)
        W_qkv = jax.random.normal(ks[1], (3 * D, D), jnp.float32) * 0.02
        b_qkv = jnp.zeros((3 * D,), jnp.float32)
        W_gate = jax.random.normal(ks[2], (N_EXP, D), jnp.float32) * 0.02
        b_gate = jnp.zeros((N_EXP,), jnp.float32)
        A = jax.random.normal(ks[3], (N_EXP, RANK, D), jnp.float32) * 0.02
        B_lora = jax.random.normal(ks[4], (N_EXP, 3 * D, RANK), jnp.float32) * 0.02
        W_proj = jax.random.normal(ks[5], (D, D), jnp.float32) * 0.02
        b_proj = jnp.zeros((D,), jnp.float32)
        return {'x': x, 'W_qkv': W_qkv, 'b_qkv': b_qkv, 'W_gate': W_gate, 'b_gate': b_gate, 'A': A, 'B_lora': B_lora, 'W_proj': W_proj, 'b_proj': b_proj}
    _L0_ffn_all = _L0_ffn_setup()
    _L0_ffn_in = {k: v for k, v in _L0_ffn_all.items() if k in ('W_qkv', 'b_qkv', 'W_gate', 'b_gate', 'A', 'B_lora', 'W_proj', 'b_proj')}
    del _L0_ffn_all
    return {'x': x, 'L0_tok_W': _L0_tok_in['W'], 'L0_tok_b': _L0_tok_in['b'], 'L0_attn_Wq': _L0_attn_in['Wq'], 'L0_attn_Wk': _L0_attn_in['Wk'], 'L0_attn_Wv': _L0_attn_in['Wv'], 'L0_ffn_W_qkv': _L0_ffn_in['W_qkv'], 'L0_ffn_b_qkv': _L0_ffn_in['b_qkv'], 'L0_ffn_W_gate': _L0_ffn_in['W_gate'], 'L0_ffn_b_gate': _L0_ffn_in['b_gate'], 'L0_ffn_A': _L0_ffn_in['A'], 'L0_ffn_B_lora': _L0_ffn_in['B_lora'], 'L0_ffn_W_proj': _L0_ffn_in['W_proj'], 'L0_ffn_b_proj': _L0_ffn_in['b_proj']}

def reference(x, L0_tok_W, L0_tok_b, L0_attn_Wq, L0_attn_Wk, L0_attn_Wv, L0_ffn_W_qkv, L0_ffn_b_qkv, L0_ffn_W_gate, L0_ffn_b_gate, L0_ffn_A, L0_ffn_B_lora, L0_ffn_W_proj, L0_ffn_b_proj):
    import jax
    import jax.numpy as jnp

    def _L0_tok_ref(x, W, b):
        import jax, jax.numpy as jnp
        import numpy as np
        CHANNELS = 90
        PATCH = 16
        EMBED = 192
        B, C, T = x.shape
        n = T // PATCH
        patches = x[:, :, :n * PATCH].reshape(B, C, n, PATCH)
        patches = patches.transpose(0, 2, 1, 3).reshape(B, n, C * PATCH)
        return jnp.einsum('bnf,ef->bne', patches, W) + b

    def _L0_attn_ref(x, Wq, Wk, Wv):
        import jax, jax.numpy as jnp
        import numpy as np
        B, S, D, H = (8, 512, 192, 192)
        q = jnp.einsum('bsd,dh->bsh', x, Wq)
        k = jnp.einsum('bsd,dh->bsh', x, Wk)
        v = jnp.einsum('bsd,dh->bsh', x, Wv)
        S_len = x.shape[-2]
        scores = jnp.einsum('bqh,bkh->bqk', q, k)
        tril = jnp.tril(jnp.ones((S_len, S_len), dtype=jnp.float32))
        scores = jnp.where(tril == 0, -jnp.inf, scores)
        attn = jax.nn.softmax(scores, axis=-1)
        return jnp.einsum('bqk,bkh->bqh', attn, v)

    def _L0_ffn_ref(x, W_qkv, b_qkv, W_gate, b_gate, A, B_lora, W_proj, b_proj):
        import jax, jax.numpy as jnp
        import numpy as np
        B_SZ, S, D = (8, 128, 192)
        H = 12
        N_EXP = 8
        RANK = 16
        ALPHA = 32
        TOP_K = 2
        b, s, d = x.shape
        n_exp, rank = (A.shape[0], A.shape[1])
        scaling = ALPHA / rank
        head_dim = d // H
        scale = head_dim ** (-0.5)
        t = b * s
        x_flat = x.reshape(t, d)
        qkv_base = x @ W_qkv.T + b_qkv
        logits = x_flat @ W_gate.T + b_gate
        router_probs = jax.nn.softmax(logits, axis=-1)
        top_k_weights, top_k_indices = jax.lax.top_k(router_probs, TOP_K)
        a_down = jnp.einsum('td,nrd->tnr', x_flat, A)
        expert_out = jnp.einsum('tnr,nor->tno', a_down, B_lora) * scaling
        dispatch = jnp.zeros((t, n_exp), x.dtype).at[jnp.arange(t)[:, None], top_k_indices].add(top_k_weights)
        sparse_out = jnp.einsum('tno,tn->to', expert_out, dispatch)
        qkv = qkv_base + sparse_out.reshape(b, s, 3 * d)
        qkv = qkv.reshape(b, s, 3, H, head_dim).transpose(2, 0, 3, 1, 4)
        q, k, v = (qkv[0], qkv[1], qkv[2])
        attn = jax.nn.softmax(jnp.einsum('bhqd,bhkd->bhqk', q, k) * scale, axis=-1)
        out = jnp.einsum('bhqk,bhkd->bhqd', attn, v)
        out = out.transpose(0, 2, 1, 3).reshape(b, s, d)
        return out @ W_proj.T + b_proj
    h = _L0_tok_ref(x, L0_tok_W, L0_tok_b)
    h = h + _L0_attn_ref(_layernorm(h, axis=-1), L0_attn_Wq, L0_attn_Wk, L0_attn_Wv)
    h = h + _L0_ffn_ref(_layernorm(h, axis=-1), L0_ffn_W_qkv, L0_ffn_b_qkv, L0_ffn_W_gate, L0_ffn_b_gate, L0_ffn_A, L0_ffn_B_lora, L0_ffn_W_proj, L0_ffn_b_proj)
    return h

_drawn_inputs = setup_inputs


def setup_inputs(seed=0):
    import zlib

    import numpy as np

    out = dict(_drawn_inputs(seed))
    spreads = {'L0_ffn_b_qkv': (0.0, 0.355), 'L0_ffn_b_gate': (0.0, 0.8), 'L0_ffn_b_proj': (0.0, 0.1)}
    factors = {'L0_ffn_W_qkv': 3.506, 'L0_ffn_W_gate': 8.0, 'L0_ffn_A': 8.0, 'L0_ffn_B_lora': 8.0}
    for name, (base, spread) in spreads.items():
        noise = np.random.default_rng([zlib.crc32(name.encode()), seed]).standard_normal(out[name].shape)
        drawn = base * np.exp(spread * noise) if base else spread * noise
        out[name] = jnp.asarray(drawn.astype(out[name].dtype))
    for name, factor in factors.items():
        out[name] = (out[name] * factor).astype(out[name].dtype)
    return out
```

```python
import concourse.bass as bass
from concourse import mybir
from contextlib import ExitStack

F32 = mybir.dt.float32
F16 = mybir.dt.float16
ALU = mybir.AluOpType
ACT = mybir.ActivationFunctionType
AX_X = mybir.AxisListType.X

B, C, T = 128, 90, 750
PATCH = 16
NT = T // PATCH
D = 192
DH = D // 2
HEADS, HD = 12, 16
N_EXP, RANK = 8, 16
NR = N_EXP * RANK
LN_EPS = 1e-5
LORA_SCALE = 2.0

GB = 8
GROUPS = B // GB
TG = GB * NT
PAIRS = GB // 2
PT_ = 2 * NT
HALF_T = TG // 2
TILES = [(0, 128), (128, 128), (256, TG - 256)]
MAIN = 12
XROW = 96
BLOCKS = [(0, 32), (32, 32), (64, C - 64)]
EXTRA = PATCH - MAIN
SLOT = 64
PAD = 128 - PT_

WS = 256.0
QS = 16.0
VS = 16.0
HSCALE = HD ** -0.5

SPLIT, TOK, ATT, MIX, HDS = 0, 1, 2, 3, 4
STEPS = GROUPS + HDS
PEELED = HDS + 2

RING = [("g0", ATT), ("g1", ATT), ("ga0", MIX), ("v0", ATT), ("ga1", MIX), ("v1", ATT),
        ("pv0", HDS), ("sc", ATT), ("at", MIX), ("pv1", HDS), ("qk0", MIX), ("pt", ATT),
        ("qk1", MIX), ("qk2", MIX), ("pv2", HDS), ("cv0", MIX), ("cv1", MIX), ("av0", ATT),
        ("av1", ATT), ("pv3", HDS), ("ot0", HDS), ("ot1", HDS), ("x2t0", ATT), ("pr0", HDS),
        ("pr1", HDS), ("x2t1", ATT), ("xt0", TOK), ("xt1", TOK)]
RING_AT = {name: n % 3 for n, (name, _) in enumerate(RING)}

TOP_LINKS = 18
TOP_SHIFTED = 3


def audio_tower(nc, x, tok_W, tok_b, Wq, Wk, Wv, W_qkv, b_qkv, W_gate, b_gate, A, B_lora,
                W_proj, b_proj, out, scratch):
    with ExitStack() as ctx:
        def sb(name, shape, dt=F32):
            return ctx.enter_context(nc.sbuf_tensor(name, shape, dt))

        def sem(name):
            return ctx.enter_context(nc.semaphore(name))

        ident = sb("ident", [128, 128])
        mask = sb("mask", [PT_, PT_])
        rank_row = sb("rank_row", [PT_, PAIRS, N_EXP])
        minus_half = sb("minus_half", [128, 4])
        eps = sb("eps", [128, 4])
        carrier = sb("carrier", [1, 1])
        w_tok = sb("w_tok", [128, 2, MAIN, D], F16)
        w_m = sb("w_m", [DH, 2, 2, D], F16)
        w_v1 = sb("w_v1", [DH, 2, 2, D], F16)
        w_ga = sb("w_ga", [DH, 2, 2, NR + N_EXP], F16)
        w_qk = sb("w_qk", [DH, 2, 2, 2 * D], F16)
        w_v2 = sb("w_v2", [DH, 2, 2, D], F16)
        w_lora = sb("w_lora", [NR, 2, 3 * D], F16)
        w_pr = sb("w_pr", [DH, 2, 2, D], F16)
        b_tok_bc = sb("b_tok_bc", [128, D])
        b_v = sb("b_v", [DH, 2])
        b_pr_bc = sb("b_pr_bc", [PT_, D])
        b_gate_bc = sb("b_gate_bc", [PT_, N_EXP])
        b_qk = sb("b_qk", [128, 3])
        raw = sb("raw", [C, 2, GB // 2, NT * PATCH])
        xs = sb("xs", [128, 2, 2, MAIN, TG], F16)
        xe = sb("xe", [C, 2, EXTRA, TG], F16)
        h = sb("h", [128, 3, D])
        st1 = sb("st1", [128, 3, 6])
        mv1 = sb("mv1", [128, 3, 2])
        ve1 = sb("ve1", [128, 3])
        rs1 = sb("rs1", [128, 3])
        xn = sb("xn", [128, 3, D])
        xnT = sb("xnT", [DH, 2, 2, 2, TG + PAD], F16)
        hp = sb("hp", [PT_, 2, PAIRS, D])
        gT = sb("gT", [DH, 2, 2, TG], F16)
        v1 = sb("v1", [PT_, PAIRS, D])
        sm = sb("sm", [PT_, PAIRS, PT_])
        m1 = sb("m1", [PT_, PAIRS])
        nm1 = sb("nm1", [PT_, PAIRS])
        p1 = sb("p1", [PT_, PAIRS, PT_])
        l1 = sb("l1", [PT_, PAIRS])
        rl1 = sb("rl1", [PT_, PAIRS])
        p1T = sb("p1T", [PT_, PAIRS, PT_])
        h2 = sb("h2", [PT_, 2, PAIRS, D])
        st2 = sb("st2", [PT_, PAIRS, 6])
        mv2 = sb("mv2", [PT_, PAIRS, 2])
        ve2 = sb("ve2", [PT_, PAIRS])
        rs2 = sb("rs2", [PT_, PAIRS])
        xn2 = sb("xn2", [PT_, PAIRS, D])
        x2T = sb("x2T", [DH, 2, 2, 2, TG], F16)
        ga = sb("ga", [PT_, PAIRS, NR + N_EXP])
        lg = sb("lg", [PT_, PAIRS, N_EXP])
        lg2 = sb("lg2", [PT_, PAIRS, N_EXP])
        key = sb("key", [PT_, 2, PAIRS, N_EXP])
        hot = sb("hot", [PT_, 2, PAIRS, N_EXP])
        top = sb("top", [PT_, 2, PAIRS])
        best = sb("best", [PT_, 2, PAIRS])
        lgm = sb("lgm", [PT_, PAIRS, N_EXP])
        pe_x = sb("pe_x", [PT_, PAIRS, N_EXP])
        pe_s = sb("pe_s", [PT_, PAIRS])
        pe_r = sb("pe_r", [PT_, PAIRS])
        both = sb("both", [PT_, PAIRS, N_EXP])
        disp0 = sb("disp0", [PT_, PAIRS, N_EXP])
        disp = sb("disp", [PT_, PAIRS, N_EXP])
        ad = sb("ad", [PT_, PAIRS, NR])
        adT = sb("adT", [NR, 2, TG], F16)
        qk = sb("qk", [128, 2, 3, TG], F16)
        v2s = sb("v2s", [PT_, 2, 2, 2, PAIRS // 2, HEADS // 2, HD + 1], F16)
        h2b = sb("h2b", [PT_, 2, PAIRS, D])
        q3 = sb("q3", [128, HEADS, TG + PAD], F16)
        k3 = sb("k3", [128, HEADS, TG], F16)
        v2_flat = sb("v2", [128, 2 * 2 * 2 * 2 * PAIRS * HEADS // 2 * (HD + 1)], F16)
        v2 = v2_flat[:].rearrange("p (a b c d e f g) -> p a b c d e f g", a=2, b=2, c=2, d=2, e=PAIRS, f=HEADS // 2)
        mx = sb("mx", [128, HEADS])
        df = sb("df", [128, HEADS, NT])
        p2 = sb("p2", [128, HEADS, SLOT])
        p2T = sb("p2T", [128, 2, HEADS // 2, 128], F16)
        rc = sb("rc", [128, HEADS])
        o2 = sb("o2", [128, PAIRS, D])
        o2T = sb("o2T", [DH, 2, 2, TG], F16)

        v2_room = v2_flat[:].bitcast(F32)
        st_tok = v2_room[0:DH, 0:2 * C * PATCH]
        q_room = q3[:].rearrange("p a b -> p (a b)").bitcast(F32)
        k_room = k3[:].rearrange("p a b -> p (a b)").bitcast(F32)
        st_q = q_room[0:DH, 0:2 * D]
        st_k = q_room[0:DH, 2 * D:4 * D]
        st_v = q_room[0:DH, 4 * D:6 * D]
        st_pr = q_room[0:DH, 6 * D:8 * D]
        st_a = q_room[0:NR, 8 * D:9 * D]
        st_g = q_room[0:N_EXP, 9 * D:10 * D]
        st_qkv = k_room[0:DH, 0:6 * D]
        st_b = k_room[0:DH, 6 * D:6 * D + 6 * NR]
        qk_T = p2T[0:DH].rearrange("p a b c -> p (a b c)").bitcast(F32)
        bias_v = o2T[:, :, :, 0:PT_]
        ps_tok = ctx.enter_context(nc.psum_tensor("ps_tok", [128, 512], F32))
        ps_s = ctx.enter_context(nc.psum_tensor("ps_s", [128, 2, 512], F32))
        ps_p = ctx.enter_context(nc.psum_tensor("ps_p", [128, 2, 512], F32))
        ps_r = ctx.enter_context(nc.psum_tensor("ps_r", [128, 3, 512], F32))

        s_w = sem("weights_loaded")
        s_ident = sem("ident_ready")
        s_zero = sem("pads_cleared")
        s_maskf = sem("mask_ready")
        s_ut = sem("unit_transposed")
        s_uh = sem("unit_high_ready")
        s_ul = sem("unit_low_ready")
        s_wd = sem("direct_weights")
        s_wz = sem("rows_and_bias_set")
        s_bv = sem("value_bias_links")
        p_bv = sem("value_bias_projected")
        s_x = [sem("x_loaded_0"), sem("x_loaded_1")]
        s_xrow = sem("extra_rows_moved")
        s_hp = sem("h_in_pairs")
        s_scw = sem("qk_in_scratch")
        s_qk3 = sem("qk_stacked")
        s_v2 = sem("v2_placed")
        s_out = [sem("out_stored_even"), sem("out_stored_odd")]
        s_hi = sem("x_high_ready")
        s_lo = sem("x_low_ready")
        p_tok = sem("tok_done")
        p_xt = sem("xt_done")
        p_g = sem("g_done")
        p_v = sem("v_done")
        p_sc = sem("scores1_done")
        p_pt = sem("p1_transposed")
        p_av = sem("attn1_done")
        p_x2t = sem("x2t_done")
        p_ga = sem("ga_done")
        p_at = sem("ad_transposed")
        p_qk = sem("qk_done")
        p_cv = sem("v2_done")
        p_s = sem("scores2_done")
        p_p = sem("p2_transposed")
        p_pv = sem("attn2_done")
        p_ot = sem("o2_transposed")
        p_pr = sem("proj_done")
        s_h = sem("h_ready")
        s_ln1 = sem("ln1_links")
        s_var1 = sem("var1_ready")
        s_rs1 = sem("rstd1_ready")
        s_ve1 = sem("var1_eps_ready")
        s_xn = sem("xn_ready")
        s_xnh = sem("xnT_high_ready")
        s_xnT = sem("xnT_ready")
        s_gh = sem("gT_high_ready")
        s_gT = sem("gT_ready")
        s_v1 = sem("v1_ready")
        s_sm = sem("scores1_masked")
        s_m1 = sem("max1_links")
        s_p1 = sem("p1_ready")
        s_p1T = sem("p1T_ready")
        s_rl1 = sem("sum1_inverted")
        s_h2 = sem("h2_ready")
        s_ln2 = sem("ln2_links")
        s_ve2 = sem("var2_eps_ready")
        s_rs2 = sem("rstd2_ready")
        s_xn2 = sem("xn2_ready")
        s_x2h = sem("x2T_high_ready")
        s_x2T = sem("x2T_ready")
        s_ga = sem("ga_ready")
        s_top = sem("top2_links")
        s_pex = sem("router_exp_ready")
        s_ad = sem("ad_ready")
        s_adh = sem("adT_high_ready")
        s_adT = sem("adT_ready")
        s_qkh = sem("qk_high_ready")
        s_qkl = sem("qk_low_ready")
        s_v2h = sem("v2_high_ready")
        s_v2s = sem("v2_evacuated")
        s_h2b = sem("h2b_ready")
        s_mx = sem("max2_ready")
        s_df = sem("scores2_shifted")
        s_p2 = sem("p2_ready")
        s_p2h = sem("p2T_high_ready")
        s_p2T = sem("p2T_ready")
        s_rc = sem("sum2_inverted")
        s_o2 = sem("o2_ready")
        s_oh = sem("o2T_high_ready")
        s_o2T = sem("o2T_ready")
        s_fin = sem("out_ready")

        FREED = {"g0": (s_gT, 2, 1), "g1": (s_gT, 2, 2), "v0": (s_v1, 2, 1), "v1": (s_v1, 2, 2),
                 "ga0": (s_ga, 2, 1), "ga1": (s_ga, 2, 2), "sc": (s_sm, 1, 1), "at": (s_adT, 1, 1),
                 "pt": (s_p1T, 1, 1), "av0": (s_h2, 4, 2), "av1": (s_h2, 4, 4),
                 "qk0": (s_qkl, 3, 1), "qk1": (s_qkl, 3, 2), "qk2": (s_qkl, 3, 3),
                 "cv0": (s_v2s, 2, 1), "cv1": (s_v2s, 2, 2),
                 "pv0": (s_o2, 8, 2), "pv1": (s_o2, 8, 4), "pv2": (s_o2, 8, 6), "pv3": (s_o2, 8, 8),
                 "ot0": (s_o2T, 2, 1), "ot1": (s_o2T, 2, 2), "pr0": (s_fin, 2, 1), "pr1": (s_fin, 2, 2),
                 "x2t0": (s_x2T, 2, 1), "x2t1": (s_x2T, 2, 2), "xt0": (s_xnT, 2, 1), "xt1": (s_xnT, 2, 2)}

        def runs(stage_lag, s):
            return not isinstance(s, int) or 0 <= s - stage_lag < GROUPS

        def bank(name):
            return ps_r[:, RING_AT[name], :]

        def bank_free(pe, name, s):
            at = [n for n, _ in RING].index(name)
            for back in range(1, 200):
                n = at - back
                steps_back, n = -(n // len(RING)), n % len(RING)
                prev, lag = RING[n]
                if RING_AT[prev] != RING_AT[name]:
                    continue
                if isinstance(s, int):
                    if s - steps_back < 0:
                        return
                    if not runs(lag, s - steps_back):
                        continue
                freed, per, place = FREED[prev]
                pe.wait_ge(freed, (s - lag) * per + (place - steps_back * per))
                return

        x_v = x.rearrange("b c t -> c b t")
        out_v = out.rearrange("b n d -> (b n) d").rearrange("(q r) d -> r q d", r=PT_)
        w_in = scratch.rearrange("a b (t p) n -> a p b t n", p=128)
        w_out = scratch.rearrange("a b (h d) n -> a b d h n", d=HD)


        UNITS = []

        def transposes_of(blocks):
            return [("t", at, src) for at, src in blocks]

        def heads_of(ap):
            return ap.rearrange("p (h e) -> p h e", e=HD)

        tokv = st_tok.rearrange("p (a c k) -> p a c k", a=2, k=PATCH)
        for j in range(0, MAIN, 2):
            blocks = [(D * jj + DH * e, tokv[:, e, :, j + jj]) for jj in range(2) for e in range(2)]
            UNITS.append((transposes_of(blocks), C, 2 * D, w_tok[0:C, 0, j:j + 2, :], w_tok[0:C, 1, j:j + 2, :], WS))
        for blk, (c0, n) in enumerate(BLOCKS):
            for q in range(0, EXTRA, 2):
                blocks = [(D * qq + DH * e, tokv[:, e, c0:c0 + n, MAIN + q + qq]) for qq in range(2) for e in range(2)]
                j = EXTRA * blk + q
                UNITS.append((transposes_of(blocks), n, 2 * D, w_tok[XROW:XROW + n, 0, j:j + 2, :],
                              w_tok[XROW:XROW + n, 1, j:j + 2, :], WS))
        for n, st in enumerate((st_q, st_k)):
            stv = st.rearrange("p (a c) -> p a c", a=2)
            blocks = [(D * hh + DH * ih, stv[:, ih, DH * hh:DH * hh + DH]) for hh in range(2) for ih in range(2)]
            dst = qk_T[:, 2 * D * n:2 * D * n + 2 * D]
            UNITS.append((transposes_of(blocks), DH, 2 * D, dst[:, 0:D], dst[:, D:2 * D], None))
        M_FROM = len(UNITS)
        UNITS.append(([("m", D * ih, ih) for ih in range(2)], DH, 2 * D, w_m[:, 0, :, :], w_m[:, 1, :, :], WS))
        for kh in range(2):
            qkvv = st_qkv.rearrange("p (a c) -> p a c", a=6)[:, :, DH * kh:DH * kh + DH]
            UNITS.append((transposes_of([(DH * a, qkvv[:, a, :]) for a in range(4)]), DH, 2 * D,
                          w_qk[:, 0, kh, :], w_qk[:, 1, kh, :], QS))
            for odd in range(2):
                UNITS.append((transposes_of([(DH * a, qkvv[:, 4 + a, :]) for a in range(2)]), DH, D,
                              *(heads_of(w_v2[:, part, kh, DH * odd:DH * (odd + 1)]) for part in range(2)), WS, odd))
            UNITS.append((transposes_of([(0, st_a[:, DH * kh:DH * kh + DH]), (NR, st_g[:, DH * kh:DH * kh + DH])]),
                          DH, NR + N_EXP, w_ga[:, 0, kh, :], w_ga[:, 1, kh, :], WS))
            prv = st_pr.rearrange("p (a c) -> p a c", a=2)[:, :, DH * kh:DH * kh + DH]
            UNITS.append((transposes_of([(DH * a, prv[:, a, :]) for a in range(2)]), DH, D,
                          w_pr[:, 0, kh, :], w_pr[:, 1, kh, :], WS))
        bv = st_b.rearrange("p (a c) -> p a c", a=6)
        UNITS.append((transposes_of([(DH * a, bv[:, a, :]) for a in range(4)]), NR, 2 * D,
                      w_lora[:, 0, 0:2 * D], w_lora[:, 1, 0:2 * D], QS))
        for odd in range(2):
            cols = slice(2 * D + DH * odd, 2 * D + DH * (odd + 1))
            UNITS.append((transposes_of([(DH * a, bv[:, 4 + a, :]) for a in range(2)]), NR, D,
                          *(heads_of(w_lora[:, part, cols]) for part in range(2)), WS, odd))
        N_LOADS = 22
        HP_DMAS = 6

        def v2_split(n, part):
            return (v2s[:, part, n, :, :, :, 0:HD].rearrange("p s a h e -> p (s a h) e"), heads_of(bank(f"cv{n}")[0:PT_, 0:2 * D]))

        def unit_bank(n, rows, cols):
            return ps_r[0:rows, n % 3, 0:cols]

        block = ctx.enter_context(nc.Block())

        def program(engine, step):
            for s in range(PEELED):
                step(s, s % 2)
            with engine.Fori(PEELED // 2, GROUPS // 2 - 1) as i:
                step(i * 2, 0)
                step(i * 2 + 1, 1)
            for s in range(GROUPS - 2, STEPS):
                step(s, s % 2)

        @block.sync
        def _(sp):
            def load(dst, src):
                sp.dma_start(dst, src).then_inc(s_w, 16)

            def clips(g, half):
                b0 = g * GB + half * (GB // 2)
                return x_v[:, bass.ds(b0 if isinstance(g, int) else sp.snap(b0), GB // 2), 0:NT * PATCH]

            def count(value):
                return value if isinstance(value, int) else sp.snap(value)

            def load_x(src, half):
                sp.dma_start(raw[:, half, :, :], src).then_inc(s_x[half], 16)

            load(st_tok.rearrange("p (a f) -> p a f", a=2), tok_W.rearrange("(a p) f -> p a f", p=DH))
            load_x(clips(0, 0), 0)
            load_x(clips(0, 1), 1)
            for st, w in ((st_q, Wq), (st_k, Wk), (st_v, Wv), (st_pr, W_proj)):
                load(st.rearrange("p (a c) -> p a c", a=2), w.rearrange("(a p) c -> p a c", p=DH))
            load(st_qkv.rearrange("p (a c) -> p a c", a=6), W_qkv.rearrange("(a p) c -> p a c", p=DH))
            load(st_a, A.rearrange("n r d -> (n r) d"))
            load(st_g, W_gate)
            for a in range(6):
                load(st_b[:, NR * a:NR * (a + 1)].rearrange("p (n r) -> p n r", n=N_EXP),
                     B_lora[:, DH * a:DH * (a + 1), :].rearrange("n p r -> p n r"))
            row = lambda v, rows: v.rearrange("(a d) -> a d", a=1).broadcast_to([rows, v.shape[0]])
            load(b_tok_bc[:], row(tok_b, 128))
            for kh in range(2):
                load(b_v[:, kh:kh + 1], b_qkv[2 * D + DH * kh:2 * D + DH * (kh + 1)].rearrange("(p a) -> p a", a=1))
            load(b_pr_bc[:], row(b_proj, PT_))
            load(b_gate_bc[:], row(b_gate, PT_))
            for t in range(3):
                load(b_qk[:, t:t + 1], b_qkv[128 * t:128 * (t + 1)].rearrange("(p a) -> p a", a=1))

            def step(s, par):
                if runs(SPLIT, s):
                    sp.wait_ge(s_lo, s * 16 + 4)
                    for blk, (c0, n) in enumerate(BLOCKS):
                        sp.dma_start(xs[XROW:XROW + n, par, :, EXTRA * blk:EXTRA * (blk + 1), :],
                                     xe[c0:c0 + n, :, :, :]).then_inc(s_xrow, 16)
                if runs(SPLIT, s) and (not isinstance(s, int) or s + 1 < GROUPS):
                    src = clips(s + 1, 0)
                    sp.wait_ge(s_lo, s * 16 + 10)
                    load_x(src, 0)
                if runs(MIX, s):
                    g = s - MIX
                    gp = (par - MIX) % 2
                    sp.wait_ge(s_qkl, g * 3 + 3)
                    for part in range(2):
                        sp.dma_start(w_in[gp, :, part, :, :], qk[:, part, :, :]).then_inc(s_scw, 16)
                    written, read = count(g * 32 + 32), None
                    if not isinstance(s, int) or s - HDS >= 0:
                        read = count((s - HDS) * PAIRS + PAIRS)
                    sp.wait_ge(s_scw, written)
                    if read is not None:
                        sp.wait_ge(p_s, read)
                    for n, (qp, kp) in enumerate(((0, 0), (1, 0), (0, 1))):
                        sp.dma_start(q3[HD * n:HD * (n + 1), :, 0:TG], w_out[gp, qp, :, 0:HEADS, :]).then_inc(s_qk3, 16)
                        sp.dma_start(k3[HD * n:HD * (n + 1), :, :], w_out[gp, kp, :, HEADS:2 * HEADS, :]).then_inc(s_qk3, 16)
                    sp.wait_ge(s_v2s, g * 2 + 2)
                    for b in range(2):
                        for odd in range(2):
                            sp.dma_start(v2[SLOT * odd:SLOT * odd + NT, gp, b, odd].rearrange("p l (n a) h e -> p (l n) (a h e)", n=2),
                                         v2s[NT * b:NT * b + NT, :, :, odd].rearrange("p l n a h e -> p (l n) (a h e)")).then_inc(s_v2, 16)
                if runs(SPLIT, s) and (not isinstance(s, int) or s + 1 < GROUPS):
                    src = clips(s + 1, 1)
                    sp.wait_ge(s_lo, s * 16 + 16)
                    load_x(src, 1)
                if runs(TOK, s):
                    g = s - TOK
                    gp = (par - TOK) % 2
                    sp.wait_ge(s_h, g * 3 + 3)
                    for p in range(PAIRS):
                        at = p * PT_
                        while at < (p + 1) * PT_:
                            t = min(at // 128, 2)
                            n = min((t + 1) * 128, (p + 1) * PT_) - at
                            sp.dma_start(hp[at - p * PT_:at - p * PT_ + n, gp, p, :],
                                         h[at - 128 * t:at - 128 * t + n, t, :]).then_inc(s_hp, 16)
                            at += n
                if runs(HDS, s):
                    g = s - HDS
                    first = g * PAIRS if isinstance(g, int) else sp.snap(g * PAIRS)
                    sp.wait_ge(s_fin, g * 2 + 2)
                    sp.dma_start(out_v[:, bass.ds(first, PAIRS), :],
                                 h2b[:, (par - HDS) % 2, :, :]).then_inc(s_out[(par - HDS) % 2], 16)

            program(sp, step)
            for parity in range(2):
                sp.wait_ge(s_out[parity], GROUPS // 2 * 16)

        @block.gpsimd
        def _(pool):
            nc.gpsimd.memset(ident[:], 0.0).then_inc(s_zero, 1)
            pool.wait_ge(s_zero, 1)
            nc.gpsimd.affine_select(out=ident[:], in_=ident[:], compare_op=ALU.not_equal, fill=1.0, base=0,
                                    pattern=[[-1, 128]], channel_multiplier=1).then_inc(s_ident, 1)
            nc.gpsimd.memset(mask[:], 0.0).then_inc(s_zero, 1)
            pool.wait_ge(s_zero, 2)
            nc.gpsimd.affine_select(out=mask[:], in_=mask[:], compare_op=ALU.is_ge, fill=-3e38, base=0,
                                    pattern=[[-1, PT_]], channel_multiplier=1).then_inc(s_zero, 1)
            pool.wait_ge(s_zero, 3)
            nc.gpsimd.affine_select(out=mask[:, 0:NT], in_=mask[:, 0:NT], compare_op=ALU.is_ge, fill=-3e38,
                                    base=NT - 1, pattern=[[0, NT]], channel_multiplier=-1).then_inc(s_maskf, 1)
            nc.gpsimd.memset(minus_half[:], -0.5).then_inc(s_maskf, 1)
            nc.gpsimd.memset(eps[:], LN_EPS).then_inc(s_maskf, 1)
            for e in range(N_EXP):
                nc.gpsimd.memset(rank_row[:, :, e:e + 1], float(N_EXP - e)).then_inc(s_maskf, 1)
            nc.gpsimd.memset(xnT[:, :, :, :, TG:TG + PAD], 0.0).then_inc(s_maskf, 1)
            nc.gpsimd.memset(p2[:, :, NT:SLOT], 0.0).then_inc(s_maskf, 1)
            nc.gpsimd.memset(v2s[:, 0, :, :, :, :, HD:HD + 1], 1.0).then_inc(s_maskf, 1)
            nc.gpsimd.memset(v2s[:, 1, :, :, :, :, HD:HD + 1], 0.0).then_inc(s_maskf, 1)
            pool.wait_ge(s_maskf, 15)
            nc.gpsimd.memset(xs[64:128, :, :, :, :], 0.0).then_inc(s_maskf, 1)
            pool.wait_ge(s_maskf, 16)

            def low_of_x(s, par, n):
                raw_v = raw[:].rearrange("p f b (n k) -> p f (b n) k", k=PATCH)
                if n < 4:
                    half, ph = n // 2, MAIN + 2 * (n % 2)
                    hi = xe[:, 0, ph - MAIN:ph - MAIN + 2, HALF_T * half:HALF_T * (half + 1)]
                    lo = xe[:, 1, ph - MAIN:ph - MAIN + 2, HALF_T * half:HALF_T * (half + 1)]
                    need = half + 1
                else:
                    half, ph = (n - 4) // 6, 2 * ((n - 4) % 6)
                    hi = xs[0:C, par, 0, ph:ph + 2, HALF_T * half:HALF_T * (half + 1)]
                    lo = xs[0:C, par, 1, ph:ph + 2, HALF_T * half:HALF_T * (half + 1)]
                    need = 2 + 3 * half + (ph // 4) + 1
                pool.wait_ge(s_hi, s * 8 + need)
                nc.gpsimd.tensor_tensor(lo, raw_v[:, half, :, ph:ph + 2].rearrange("p t k -> p k t"),
                                        hi, ALU.subtract).then_inc(s_lo, 1)

            def rstd(ready, count, src, dst, ve, ve_sem, done, n_done):
                rows, cols = ve.shape[0], ve.shape[1]
                pool.wait_ge(ready, count)
                nc.gpsimd.tensor_tensor(ve, src, eps[0:rows, 0:cols], ALU.add).then_inc(ve_sem, 1)
                pool.wait_ge(ve_sem, n_done)
                nc.gpsimd.tensor_tensor(dst, ve, minus_half[0:rows, 0:cols], ALU.pow).then_inc(done, 1)
                pool.wait_ge(done, n_done)

            def step(s, par):
                def lows(a, b):
                    if runs(SPLIT, s):
                        for n in range(a, b):
                            low_of_x(s, par, n)

                def ln1(t):
                    if runs(TOK, s):
                        g, m = s - TOK, TILES[t][1]
                        rstd(s_var1, g * 3 + (t + 1), mv1[0:m, t, 1:2], rs1[0:m, t:t + 1],
                             ve1[0:m, t:t + 1], s_ve1, s_rs1, g * 3 + (t + 1))

                def low_is_done(n):
                    if runs(SPLIT, s):
                        pool.wait_ge(s_lo, s * 16 + n)

                lows(0, 4)
                if runs(MIX, s):
                    g = s - MIX
                    low_is_done(4)
                    pool.wait_ge(s_top, g * TOP_LINKS + TOP_LINKS)
                    nc.gpsimd.tensor_tensor(ad[:].rearrange("p a (n r) -> p a n r", n=N_EXP),
                                            ga[:, :, 0:NR].rearrange("p a (n r) -> p a n r", n=N_EXP),
                                            disp[:].unsqueeze(3).to_broadcast([PT_, PAIRS, N_EXP, RANK]),
                                            ALU.mult).then_inc(s_ad, 1)
                    pool.wait_ge(s_ad, g + 1)
                lows(4, 7)
                low_is_done(7)
                ln1(0)
                if runs(MIX, s):
                    g = s - MIX
                    gp = (par - MIX) % 2
                    pool.wait_ge(s_xn2, g * PAIRS + PAIRS)
                    if not isinstance(s, int) or g >= 2:
                        pool.wait_ge(s_out[gp], (g - gp) * 8)
                    nc.gpsimd.tensor_tensor(h2b[:, gp, :, :], h2[:, gp, :, :],
                                            b_pr_bc[:].unsqueeze(1).to_broadcast([PT_, PAIRS, D]),
                                            ALU.add).then_inc(s_h2b, 1)
                    pool.wait_ge(s_h2b, g + 1)
                lows(7, 13)
                if runs(ATT, s):
                    g = s - ATT
                    low_is_done(13)
                    rstd(s_ln2, g * 5 + 5, mv2[:, :, 1], rs2[:, :], ve2[:, :], s_ve2, s_rs2, g + 1)
                lows(13, 14)
                low_is_done(14)
                ln1(1)
                lows(14, 16)
                low_is_done(16)
                ln1(2)

            program(pool, step)

        @block.scalar
        def _(act):
            def copy(out_, in_, scale=1.0):
                return nc.scalar.activation(out_, in_, ACT.Copy, scale=scale)

            act.wait_ge(s_w, 16 * N_LOADS)
            act.wait_ge(s_wz, 2)
            act.wait_ge(s_maskf, 16)
            for n, (_, rows, cols, hi, lo, scale, *odd) in enumerate(UNITS):
                act.wait_ge(s_ut, n + 1)
                src = unit_bank(n, rows, cols)
                if scale is None:
                    copy(hi, src[:, 0:D]).then_inc(s_uh, 1)
                else:
                    copy(hi, as_shape(src, hi, *odd), scale).then_inc(s_uh, 1)
            copy(w_v1[:, 0, :, :], st_v.rearrange("p (a c) -> p a c", a=2), WS).then_inc(s_wd, 1)

            def high_of_x(s, par, n):
                raw_v = raw[:].rearrange("p f b (n k) -> p f (b n) k", k=PATCH)
                half = n if n < 2 else (n - 2) // 3
                if n < 2:
                    ph = MAIN
                    hi = xe[:, 0, :, HALF_T * half:HALF_T * (half + 1)]
                    if not isinstance(s, int) or s > 0:
                        if n == 0:
                            act.wait_ge(s_xrow, s * 48)
                else:
                    ph = 4 * ((n - 2) % 3)
                    hi = xs[0:C, par, 0, ph:ph + 4, HALF_T * half:HALF_T * (half + 1)]
                act.wait_ge(s_x[half], s * 16 + 16)
                copy(hi, raw_v[:, half, :, ph:ph + 4].rearrange("p t k -> p k t")).then_inc(s_hi, 1)

            def step(s, par):
                gs = {lag: s - lag for lag in range(5)}
                gpar = {lag: (par - lag) % 2 for lag in range(5)}

                def highs(a, b):
                    if runs(SPLIT, s):
                        for n in range(a, b):
                            high_of_x(s, par, n)

                def exp2(p):
                    if runs(HDS, s):
                        act.wait_ge(s_df, gs[HDS] * PAIRS + (p + 1))
                        if p:
                            act.wait_ge(p_p, gs[HDS] * PAIRS + p)
                        nc.scalar.activation(p2[:, :, 0:NT], df[:], ACT.Exp, scale=HSCALE / (QS * QS)).then_inc(s_p2, 1)

                def p2t(p):
                    if runs(HDS, s):
                        act.wait_ge(p_p, gs[HDS] * PAIRS + (p + 1))
                        if p:
                            act.wait_ge(p_pv, gs[HDS] * PAIRS + p)
                        copy(p2T[:, 0].rearrange("p (a b) c -> p a (b c)", a=2), ps_p[:, :, 0:3 * 128]).then_inc(s_p2h, 1)

                highs(0, 2)
                if runs(ATT, s):
                    for jh in range(2):
                        act.wait_ge(p_g, gs[ATT] * 2 + (jh + 1))
                        copy(gT[:, 0, jh, :], bank(f"g{jh}")[0:DH, 0:TG], 1 / WS).then_inc(s_gh, 1)
                highs(2, 3)
                for n in range(2):
                    if runs(MIX, s):
                        act.wait_ge(p_ga, gs[MIX] * 2 + (n + 1))
                        copy(ga[:, 2 * n:2 * n + 2, :],
                             bank(f"ga{n}")[0:PT_, 0:2 * (NR + N_EXP)].rearrange("p (a c) -> p a c", a=2), 1 / WS).then_inc(s_ga, 1)
                    if n == 0:
                        exp2(0)
                    if runs(ATT, s):
                        act.wait_ge(p_v, gs[ATT] * 2 + (n + 1))
                        copy(v1[:, 2 * n:2 * n + 2, :],
                             bank(f"v{n}")[0:PT_, 0:2 * D].rearrange("p (a c) -> p a c", a=2), 1 / WS).then_inc(s_v1, 1)
                    if n == 0:
                        p2t(0)
                exp2(1)
                highs(3, 4)
                if runs(MIX, s):
                    act.wait_ge(s_top, gs[MIX] * TOP_LINKS + TOP_SHIFTED)
                    nc.scalar.activation(pe_x[:], lgm[:], ACT.Exp).then_inc(s_pex, 1)
                p2t(1)
                highs(4, 5)
                exp2(2)
                if runs(ATT, s):
                    for p in range(PAIRS):
                        act.wait_ge(s_m1, gs[ATT] * 2 + 2)
                        nc.scalar.activation(p1[:, p, :], sm[:, p, :], ACT.Exp, bias=nm1[:, p:p + 1],
                                             accum_out=l1[:, p:p + 1]).then_inc(s_p1, 1)
                if runs(MIX, s):
                    act.wait_ge(p_at, gs[MIX] + 1)
                    copy(adT[:, 0, :], bank("at")[0:NR, 0:TG]).then_inc(s_adh, 1)
                highs(5, 6)
                if runs(MIX, s):
                    act.wait_ge(p_qk, gs[MIX] * 3 + 1)
                    nc.scalar.activation(qk[:, 0, 0, :], bank("qk0")[:, 0:TG], ACT.Identity, bias=b_qk[:, 0:1]).then_inc(s_qkh, 1)
                if runs(ATT, s):
                    act.wait_ge(p_pt, gs[ATT] + 1)
                    copy(p1T[:], bank("pt")[0:PT_, 0:PAIRS * PT_].rearrange("p (a c) -> p a c", a=PAIRS)).then_inc(s_p1T, 1)
                if runs(MIX, s):
                    act.wait_ge(p_qk, gs[MIX] * 3 + 2)
                    nc.scalar.activation(qk[:, 0, 1, :], bank("qk1")[:, 0:TG], ACT.Identity, bias=b_qk[:, 1:2]).then_inc(s_qkh, 1)
                p2t(2)
                exp2(3)
                if runs(MIX, s):
                    act.wait_ge(p_qk, gs[MIX] * 3 + 3)
                    nc.scalar.activation(qk[:, 0, 2, :], bank("qk2")[:, 0:TG], ACT.Identity, bias=b_qk[:, 2:3]).then_inc(s_qkh, 1)
                highs(6, 7)
                if runs(MIX, s):
                    for n in range(2):
                        act.wait_ge(p_cv, gs[MIX] * 2 + (n + 1))
                        copy(*v2_split(n, 0), VS / WS).then_inc(s_v2h, 1)
                p2t(3)
                highs(7, 8)
                if runs(HDS, s):
                    for kh in range(2):
                        act.wait_ge(p_ot, gs[HDS] * 2 + (kh + 1))
                        copy(o2T[:, 0, kh, :].rearrange("p (a t) -> p a t", t=NT),
                             bank(f"ot{kh}")[0:DH, :].rearrange("p (a t) -> p a t", t=SLOT)[:, :, 0:NT]).then_inc(s_oh, 1)
                if runs(ATT, s):
                    for kh in range(2):
                        act.wait_ge(p_x2t, gs[ATT] * 2 + (kh + 1))
                        copy(x2T[:, gpar[ATT], 0, kh, :], bank(f"x2t{kh}")[0:DH, 0:TG]).then_inc(s_x2h, 1)
                if runs(TOK, s):
                    for kh in range(2):
                        act.wait_ge(p_xt, gs[TOK] * 2 + (kh + 1))
                        copy(xnT[:, gpar[TOK], 0, kh, 0:TG], bank(f"xt{kh}")[0:DH, 0:TG]).then_inc(s_xnh, 1)

            program(act, step)

        @block.vector
        def _(dve):
            dve.wait_ge(s_w, 16 * N_LOADS)
            nc.vector.memset(w_tok[64:128, :, :, :], 0.0).then_inc(s_wz, 1)
            nc.vector.tensor_scalar(b_qk[:], b_qk[:], QS, None, ALU.mult).then_inc(s_wz, 1)
            for n, (_, rows, cols, hi, lo, scale, *odd) in enumerate(UNITS):
                dve.wait_ge(s_uh, n + 1)
                src = unit_bank(n, rows, cols)
                if scale is None:
                    nc.vector.tensor_copy(lo, src[:, D:2 * D]).then_inc(s_ul, 1)
                else:
                    nc.vector.scalar_tensor_tensor(out=lo, in0=as_shape(src, hi, *odd), scalar=scale, in1=hi,
                                                   op0=ALU.mult, op1=ALU.subtract).then_inc(s_ul, 1)
            dve.wait_ge(s_wd, 1)
            nc.vector.scalar_tensor_tensor(out=w_v1[:, 1, :, :], in0=st_v.rearrange("p (a c) -> p a c", a=2), scalar=WS,
                                           in1=w_v1[:, 0, :, :], op0=ALU.mult, op1=ALU.subtract).then_inc(s_wd, 1)
            dve.wait_ge(s_wd, 2)
            nc.vector.memset(v2_room, 0.0).then_inc(s_wz, 1)
            nc.vector.tensor_scalar(bias_v[:, 0], b_v[:].unsqueeze(2).to_broadcast([DH, 2, PT_]), QS, None, ALU.mult).then_inc(s_bv, 1)
            dve.wait_ge(s_bv, 1)
            nc.vector.scalar_tensor_tensor(out=bias_v[:, 1], in0=b_v[:].unsqueeze(2).to_broadcast([DH, 2, PT_]), scalar=QS,
                                           in1=bias_v[:, 0], op0=ALU.mult, op1=ALU.subtract).then_inc(s_bv, 1)
            dve.wait_ge(p_bv, 1)
            nc.vector.scalar_tensor_tensor(out=b_pr_bc[:], in0=unit_bank(len(UNITS), PT_, D), scalar=1 / (WS * QS),
                                           in1=b_pr_bc[:], op0=ALU.mult, op1=ALU.add).then_inc(s_bv, 1)
            dve.wait_ge(s_wz, 3)
            nc.vector.memset(q3[0:3 * HD, :, TG:], 0.0).then_inc(s_wz, 1)

            def step(s, par):
                gs = {lag: s - lag for lag in range(5)}
                gpar = {lag: (par - lag) % 2 for lag in range(5)}

                def low(out_, src, hi, scale, ready, count, done):
                    dve.wait_ge(ready, count)
                    nc.vector.scalar_tensor_tensor(out=out_, in0=src, scalar=scale, in1=hi,
                                                   op0=ALU.mult, op1=ALU.subtract).then_inc(done, 1)

                def shift(p):
                    if runs(HDS, s):
                        n = gs[HDS] * PAIRS + (p + 1)
                        sc = ps_s[:, :, 0:6 * NT].rearrange("p a (h k) -> p a h k", k=NT)
                        dve.wait_ge(p_s, n)
                        nc.vector.tensor_reduce(mx[:].rearrange("p (a h) -> p a h", a=2), sc, AX_X, ALU.max).then_inc(s_mx, 1)
                        dve.wait_ge(s_mx, n)
                        if p:
                            dve.wait_ge(s_p2, gs[HDS] * PAIRS + p)
                        nc.vector.tensor_tensor(df[:].rearrange("p (a h) k -> p a h k", a=2), sc,
                                                mx[:].rearrange("p (a h) -> p a h", a=2).unsqueeze(3).to_broadcast([128, 2, 6, NT]),
                                                ALU.subtract).then_inc(s_df, 1)

                def p2t(p):
                    if runs(HDS, s):
                        low(p2T[:, 1].rearrange("p (a b) c -> p a (b c)", a=2), ps_p[:, :, 0:3 * 128],
                            p2T[:, 0].rearrange("p (a b) c -> p a (b c)", a=2), 1.0, s_p2h, gs[HDS] * PAIRS + (p + 1), s_p2T)

                def norm2(p):
                    if runs(HDS, s):
                        dve.wait_ge(p_pv, gs[HDS] * PAIRS + (p + 1))
                        pv = bank(f"pv{p}")[:, 0:HEADS * 2 * (HD + 1)].rearrange("p (h b e) -> p h b e", h=HEADS, b=2)
                        for b in range(2):
                            r = slice(SLOT * b, SLOT * (b + 1))
                            nc.vector.reciprocal(rc[r, :], pv[r, :, b, HD]).then_inc(s_rc, 1)
                        for b in range(2):
                            r = slice(SLOT * b, SLOT * (b + 1))
                            dve.wait_ge(s_rc, gs[HDS] * PAIRS * 2 + (2 * p + 1 + b))
                            nc.vector.tensor_tensor(o2[r, p, :].rearrange("p (h e) -> p h e", h=HEADS), pv[r, :, b, 0:HD],
                                                    rc[r, :].unsqueeze(2).to_broadcast([SLOT, HEADS, HD]),
                                                    ALU.mult).then_inc(s_o2, 1)

                def h_tile(t):
                    if runs(TOK, s):
                        g, m = gs[TOK], TILES[t][1]
                        n = g * 3 + (t + 1)
                        dve.wait_ge(p_tok, n)
                        if t == 0 and (not isinstance(s, int) or s > TOK):
                            dve.wait_ge(s_hp, g * 16 * HP_DMAS)
                        nc.vector.scalar_tensor_tensor(out=h[0:m, t, :], in0=ps_tok[0:m, 0:D], scalar=1 / WS,
                                                       in1=b_tok_bc[0:m, :], op0=ALU.mult, op1=ALU.add).then_inc(s_h, 1)
                        dve.wait_ge(s_h, n)
                        nc.vector.bn_stats(st1[0:m, t, :], h[0:m, t, :]).then_inc(s_ln1, 1)
                        dve.wait_ge(s_ln1, n)
                        nc.vector.memset(carrier[:], 0.0)
                        nc.vector.bn_aggr(mv1[0:m, t, :], st1[0:m, t, :]).then_inc(s_var1, 1)

                def xn_tile(t):
                    if runs(TOK, s):
                        g, m = gs[TOK], TILES[t][1]
                        dve.wait_ge(s_rs1, g * 3 + (t + 1))
                        nc.vector.tensor_scalar(xn[0:m, t, :], h[0:m, t, :], mv1[0:m, t, 0:1], rs1[0:m, t:t + 1],
                                                ALU.subtract, ALU.mult).then_inc(s_xn, 1)

                def top2():
                    g = gs[MIX]
                    links = [0]

                    def link(ins):
                        links[0] += 1
                        ins.then_inc(s_top, 1)
                        dve.wait_ge(s_top, g * TOP_LINKS + links[0])

                    def per_pair(ap):
                        return ap.unsqueeze(2).to_broadcast([PT_, PAIRS, N_EXP])

                    dve.wait_ge(s_ga, g * 2 + 2)
                    link(nc.vector.tensor_tensor(lg[:], ga[:, :, NR:NR + N_EXP],
                                                 b_gate_bc[:].unsqueeze(1).to_broadcast([PT_, PAIRS, N_EXP]), ALU.add))
                    for k, src in enumerate((lg, lg2)):
                        link(nc.vector.tensor_reduce(top[:, k, :], src[:], AX_X, ALU.max))
                        if k == 0:
                            link(nc.vector.tensor_tensor(lgm[:], lg[:], per_pair(top[:, 0, :]), ALU.subtract))
                            assert links[0] == TOP_SHIFTED
                        link(nc.vector.tensor_tensor(key[:, k, :, :], src[:], per_pair(top[:, k, :]), ALU.is_equal))
                        link(nc.vector.tensor_tensor(hot[:, k, :, :], key[:, k, :, :], rank_row[:], ALU.mult))
                        link(nc.vector.tensor_reduce(best[:, k, :], hot[:, k, :, :], AX_X, ALU.max))
                        link(nc.vector.tensor_tensor(key[:, k, :, :], hot[:, k, :, :], per_pair(best[:, k, :]), ALU.is_equal))
                        if k == 0:
                            link(nc.vector.scalar_tensor_tensor(out=lg2[:], in0=key[:, 0, :, :], scalar=-3e38, in1=lg[:],
                                                                op0=ALU.mult, op1=ALU.add))
                    return link, per_pair

                if runs(HDS, s):
                    shift(0)
                if runs(ATT, s):
                    for jh in range(2):
                        low(gT[:, 1, jh, :], bank(f"g{jh}")[0:DH, 0:TG], gT[:, 0, jh, :], 1 / WS, s_gh, gs[ATT] * 2 + (jh + 1), s_gT)
                shift(1)
                p2t(0)
                if runs(MIX, s):
                    link, per_pair = top2()
                    link(nc.vector.tensor_tensor(both[:], key[:, 0, :, :], key[:, 1, :, :], ALU.add))
                    dve.wait_ge(s_pex, gs[MIX] + 1)
                    link(nc.vector.tensor_reduce(pe_s[:], pe_x[:], AX_X, ALU.add))
                    link(nc.vector.reciprocal(pe_r[:], pe_s[:]))
                    link(nc.vector.scalar_tensor_tensor(out=disp0[:], in0=both[:], scalar=LORA_SCALE, in1=pe_x[:],
                                                        op0=ALU.mult, op1=ALU.mult))
                    nc.vector.tensor_tensor(disp[:], disp0[:], per_pair(pe_r[:]), ALU.mult).then_inc(s_top, 1)
                norm2(0)
                h_tile(0)
                if runs(ATT, s):
                    g = gs[ATT]
                    dve.wait_ge(p_sc, g + 1)
                    nc.vector.tensor_tensor(sm[:], bank("sc")[0:PT_, :].rearrange("p (a c) -> p a c", a=PAIRS)[:, :, 0:PT_],
                                            mask[:].unsqueeze(1).to_broadcast([PT_, PAIRS, PT_]), ALU.add).then_inc(s_sm, 1)
                    dve.wait_ge(s_sm, g + 1)
                    nc.vector.tensor_reduce(m1[:], sm[:], AX_X, ALU.max).then_inc(s_m1, 1)
                    dve.wait_ge(s_m1, g * 2 + 1)
                    nc.vector.tensor_scalar(nm1[:], m1[:], -1.0, None, ALU.mult).then_inc(s_m1, 1)
                shift(2)
                p2t(1)
                if runs(MIX, s):
                    low(adT[:, 1, :], bank("at")[0:NR, 0:TG], adT[:, 0, :], 1.0, s_adh, gs[MIX] + 1, s_adT)
                norm2(1)

                def qk_low(t):
                    if runs(MIX, s):
                        dve.wait_ge(s_qkh, gs[MIX] * 3 + (t + 1))
                        nc.vector.scalar_tensor_tensor(out=qk[:, 1, t, :], in0=bank(f"qk{t}")[:, 0:TG], scalar=b_qk[:, t:t + 1],
                                                       in1=qk[:, 0, t, :], op0=ALU.add, op1=ALU.subtract).then_inc(s_qkl, 1)

                qk_low(0)
                shift(3)
                xn_tile(0)
                if runs(ATT, s):
                    dve.wait_ge(s_p1, gs[ATT] * PAIRS + PAIRS)
                    nc.vector.reciprocal(rl1[:], l1[:]).then_inc(s_rl1, 1)
                qk_low(1)
                p2t(2)
                qk_low(2)
                norm2(2)
                if runs(MIX, s):
                    for n in range(2):
                        lo_, src = v2_split(n, 1)
                        low(lo_, src, v2_split(n, 0)[0], VS / WS, s_v2h, gs[MIX] * 2 + (n + 1), s_v2s)
                p2t(3)
                if runs(ATT, s):
                    g, gp = gs[ATT], gpar[ATT]
                    dve.wait_ge(s_rl1, g + 1)
                    dve.wait_ge(s_hp, (g + 1) * 16 * HP_DMAS)
                    for p in range(PAIRS):
                        dve.wait_ge(p_av, g * 2 + (p // 2 + 1))
                        nc.vector.scalar_tensor_tensor(out=h2[:, gp, p, :],
                                                       in0=bank(f"av{p // 2}")[0:PT_, D * (p % 2):D * (p % 2 + 1)],
                                                       scalar=rl1[:, p:p + 1], in1=hp[:, gp, p, :],
                                                       op0=ALU.mult, op1=ALU.add).then_inc(s_h2, 1)
                    for p in range(PAIRS):
                        dve.wait_ge(s_h2, g * PAIRS + (p + 1))
                        nc.vector.bn_stats(st2[:, p, :], h2[:, gp, p, :]).then_inc(s_ln2, 1)
                    dve.wait_ge(s_ln2, g * 5 + PAIRS)
                    nc.vector.memset(carrier[:], 0.0)
                    for p in range(PAIRS):
                        ins = nc.vector.bn_aggr(mv2[:, p, :], st2[:, p, :])
                    ins.then_inc(s_ln2, 1)
                h_tile(1)
                norm2(3)
                if runs(ATT, s):
                    dve.wait_ge(s_rs2, gs[ATT] + 1)
                    for p in range(PAIRS):
                        nc.vector.tensor_scalar(xn2[:, p, :], h2[:, gpar[ATT], p, :], mv2[:, p, 0:1], rs2[:, p:p + 1],
                                                ALU.subtract, ALU.mult).then_inc(s_xn2, 1)
                xn_tile(1)
                if runs(HDS, s):
                    for kh in range(2):
                        low(o2T[:, 1, kh, :].rearrange("p (a t) -> p a t", t=NT),
                            bank(f"ot{kh}")[0:DH, :].rearrange("p (a t) -> p a t", t=SLOT)[:, :, 0:NT],
                            o2T[:, 0, kh, :].rearrange("p (a t) -> p a t", t=NT), 1.0, s_oh, gs[HDS] * 2 + (kh + 1), s_o2T)

                def x2_low(kh):
                    if runs(ATT, s):
                        low(x2T[:, gpar[ATT], 1, kh, :], bank(f"x2t{kh}")[0:DH, 0:TG], x2T[:, gpar[ATT], 0, kh, :],
                            1.0, s_x2h, gs[ATT] * 2 + (kh + 1), s_x2T)

                h_tile(2)
                x2_low(0)
                if runs(HDS, s):
                    g, gp = gs[HDS], gpar[HDS]
                    dve.wait_ge(s_h2b, g + 1)
                    for n in range(2):
                        dve.wait_ge(p_pr, g * 2 + (n + 1))
                        nc.vector.scalar_tensor_tensor(out=h2b[:, gp, 2 * n:2 * n + 2, :],
                                                       in0=bank(f"pr{n}")[0:PT_, 0:2 * D].rearrange("p (a c) -> p a c", a=2),
                                                       scalar=1 / (WS * VS), in1=h2b[:, gp, 2 * n:2 * n + 2, :],
                                                       op0=ALU.mult, op1=ALU.add).then_inc(s_fin, 1)
                xn_tile(2)
                x2_low(1)
                if runs(TOK, s):
                    for kh in range(2):
                        low(xnT[:, gpar[TOK], 1, kh, 0:TG], bank(f"xt{kh}")[0:DH, 0:TG], xnT[:, gpar[TOK], 0, kh, 0:TG],
                            1.0, s_xnh, gs[TOK] * 2 + (kh + 1), s_xnT)

            program(dve, step)

        @block.tensor
        def _(pe):
            mm = nc.tensor.matmul

            def split_product(dst, stat, mov, start, stop):
                mm(dst, stat[0], mov[0], start=start, stop=False)
                mm(dst, stat[0], mov[1], start=False, stop=False)
                return mm(dst, stat[1], mov[0], start=False, stop=stop)

            pe.wait_ge(s_w, 16 * N_LOADS)
            pe.wait_ge(s_ident, 1)
            for n, (parts, rows, cols, *_) in enumerate(UNITS):
                if n >= 3:
                    pe.wait_ge(s_ul, n - 2)
                if n == M_FROM:
                    pe.wait_ge(s_ul, n)
                for kind, at, src in parts:
                    if kind == "t":
                        k, m = src.shape[0], src.shape[1]
                        last = nc.tensor.transpose(unit_bank(n, rows, cols)[:, at:at + k], src, ident[0:k, 0:k])
                    else:
                        for hh in range(2):
                            last = mm(unit_bank(n, rows, cols)[:, at:at + D], qk_T[:, D * hh + DH * src:D * hh + DH * src + DH],
                                      qk_T[:, 2 * D + D * hh:2 * D + D * hh + D], start=(hh == 0), stop=(hh == 1))
                last.then_inc(s_ut, 1)
            pe.wait_ge(s_ul, len(UNITS))
            pe.wait_ge(s_bv, 2)
            for kh in range(2):
                last = split_product(unit_bank(len(UNITS), PT_, D), [bias_v[:, part, kh, :] for part in range(2)],
                                     [w_pr[:, part, kh, :] for part in range(2)], kh == 0, kh == 1)
            last.then_inc(p_bv, 1)
            pe.wait_ge(s_bv, 3)
            pe.wait_ge(s_wd, 2)
            pe.wait_ge(s_maskf, 16)
            pe.wait_ge(s_wz, 4)

            def step(s, par):
                gs = {lag: s - lag for lag in range(5)}
                gpar = {lag: (par - lag) % 2 for lag in range(5)}

                def tok(k):
                    if not runs(TOK, s):
                        return
                    g, gp = gs[TOK], gpar[TOK]
                    t, q = k // 4, k % 4
                    t0, m = TILES[t]
                    if k == 0:
                        pe.wait_ge(s_lo, g * 16 + 16)
                        pe.wait_ge(s_xrow, g * 48 + 48)
                    if q == 0 and (not isinstance(s, int) or s > TOK or t > 0):
                        pe.wait_ge(s_h, g * 3 + t)
                    for j in range(3 * q, 3 * q + 3):
                        last = split_product(ps_tok[0:m, 0:D], [xs[:, gp, part, j, t0:t0 + m] for part in range(2)],
                                             [w_tok[:, part, j, :] for part in range(2)], j == 0, j == MAIN - 1)
                    if q == 3:
                        last.then_inc(p_tok, 1)

                def xt():
                    if runs(TOK, s):
                        for kh in range(2):
                            if kh == 0:
                                pe.wait_ge(s_xn, gs[TOK] * 3 + 3)
                            bank_free(pe, f"xt{kh}", s)
                            for t, (t0, m) in enumerate(TILES):
                                last = nc.tensor.transpose(bank(f"xt{kh}")[0:DH, t0:t0 + m],
                                                           xn[0:m, t, DH * kh:DH * (kh + 1)], ident[0:m, 0:m])
                            last.then_inc(p_xt, 1)

                def g_(jh):
                    if runs(ATT, s):
                        gp = gpar[ATT]
                        if jh == 0:
                            pe.wait_ge(s_xnT, gs[ATT] * 2 + 2)
                        bank_free(pe, f"g{jh}", s)
                        for kh in range(2):
                            last = split_product(bank(f"g{jh}")[0:DH, 0:TG],
                                                 [w_m[:, part, kh, DH * jh:DH * (jh + 1)] for part in range(2)],
                                                 [xnT[:, gp, part, kh, 0:TG] for part in range(2)], kh == 0, kh == 1)
                        last.then_inc(p_g, 1)

                def tokens_times(name, p, stat, mov, cols, first, stop=True):
                    dst = bank(name)[0:PT_, first:first + cols]
                    for kh in range(2):
                        last = split_product(dst, [stat(part, kh) for part in range(2)],
                                             [mov(part, kh) for part in range(2)], kh == 0, stop and kh == 1)
                    return last

                def v_(n):
                    if runs(ATT, s):
                        gp = gpar[ATT]
                        bank_free(pe, f"v{n}", s)
                        for p in (2 * n, 2 * n + 1):
                            last = tokens_times(f"v{n}", p, lambda part, kh: xnT[:, gp, part, kh, PT_ * p:PT_ * (p + 1)],
                                                lambda part, kh: w_v1[:, part, kh, :], D, D * (p % 2))
                        last.then_inc(p_v, 1)

                def sc():
                    if runs(ATT, s):
                        gp = gpar[ATT]
                        pe.wait_ge(s_gT, gs[ATT] * 2 + 2)
                        bank_free(pe, "sc", s)
                        for p in range(PAIRS):
                            last = tokens_times("sc", p, lambda part, kh: gT[:, part, kh, PT_ * p:PT_ * (p + 1)],
                                                lambda part, kh: xnT[:, gp, part, kh, PT_ * p:PT_ * p + 128], 128, 128 * p)
                        last.then_inc(p_sc, 1)

                def pt():
                    if runs(ATT, s):
                        pe.wait_ge(s_p1, gs[ATT] * PAIRS + PAIRS)
                        bank_free(pe, "pt", s)
                        for p in range(PAIRS):
                            last = nc.tensor.transpose(bank("pt")[0:PT_, PT_ * p:PT_ * (p + 1)], p1[:, p, :], ident[0:PT_, 0:PT_])
                        last.then_inc(p_pt, 1)

                def av(n):
                    if runs(ATT, s):
                        if n == 0:
                            pe.wait_ge(s_p1T, gs[ATT] + 1)
                            pe.wait_ge(s_v1, gs[ATT] * 2 + 2)
                        bank_free(pe, f"av{n}", s)
                        for p in (2 * n, 2 * n + 1):
                            last = mm(bank(f"av{n}")[0:PT_, D * (p % 2):D * (p % 2 + 1)], p1T[:, p, :], v1[:, p, :],
                                      start=True, stop=True)
                        last.then_inc(p_av, 1)

                def x2t(kh):
                    if runs(ATT, s):
                        if kh == 0:
                            pe.wait_ge(s_xn2, gs[ATT] * PAIRS + PAIRS)
                        bank_free(pe, f"x2t{kh}", s)
                        for p in range(PAIRS):
                            last = nc.tensor.transpose(bank(f"x2t{kh}")[0:DH, PT_ * p:PT_ * (p + 1)],
                                                       xn2[:, p, DH * kh:DH * (kh + 1)], ident[0:PT_, 0:PT_])
                        last.then_inc(p_x2t, 1)

                def ga_(n):
                    if runs(MIX, s):
                        gp = gpar[MIX]
                        if n == 0:
                            pe.wait_ge(s_x2T, gs[MIX] * 2 + 2)
                        bank_free(pe, f"ga{n}", s)
                        for p in (2 * n, 2 * n + 1):
                            last = tokens_times(f"ga{n}", p, lambda part, kh: x2T[:, gp, part, kh, PT_ * p:PT_ * (p + 1)],
                                                lambda part, kh: w_ga[:, part, kh, :], NR + N_EXP, (NR + N_EXP) * (p % 2))
                        last.then_inc(p_ga, 1)

                def at():
                    if runs(MIX, s):
                        pe.wait_ge(s_ad, gs[MIX] + 1)
                        bank_free(pe, "at", s)
                        for p in range(PAIRS):
                            last = nc.tensor.transpose(bank("at")[0:NR, PT_ * p:PT_ * (p + 1)], ad[:, p, :], ident[0:PT_, 0:PT_])
                        last.then_inc(p_at, 1)

                def qk_(t):
                    if runs(MIX, s):
                        gp = gpar[MIX]
                        if t == 0:
                            pe.wait_ge(s_adT, gs[MIX] + 1)
                        bank_free(pe, f"qk{t}", s)
                        dst = bank(f"qk{t}")[:, 0:TG]
                        cols = slice(128 * t, 128 * (t + 1))
                        for kh in range(2):
                            split_product(dst, [w_qk[:, part, kh, cols] for part in range(2)],
                                          [x2T[:, gp, part, kh, :] for part in range(2)], kh == 0, False)
                        split_product(dst, [w_lora[:, part, cols] for part in range(2)],
                                      [adT[:, part, :] for part in range(2)], False, True).then_inc(p_qk, 1)

                def cv(n):
                    if runs(MIX, s):
                        gp = gpar[MIX]
                        bank_free(pe, f"cv{n}", s)
                        by_half = bank(f"cv{n}")[0:PT_, 0:2 * D].rearrange("p (s a c) -> p a s c", s=2, a=2)
                        for p in (2 * n, 2 * n + 1):
                            tok_p = slice(PT_ * p, PT_ * (p + 1))
                            for kh in range(2):
                                split_product(by_half[:, p % 2], [x2T[:, gp, part, kh, tok_p] for part in range(2)],
                                              [w_v2[:, part, kh, :] for part in range(2)], kh == 0, False)
                            last = split_product(by_half[:, p % 2],
                                                 [adT[:, part, tok_p] for part in range(2)],
                                                 [w_lora[:, part, 2 * D:3 * D] for part in range(2)], False, True)
                        last.then_inc(p_cv, 1)

                def s_(p):
                    if runs(HDS, s):
                        g = gs[HDS]
                        if p == 0:
                            pe.wait_ge(s_qk3, (g + 1) * 96)
                        if p or not isinstance(s, int) or s > HDS:
                            pe.wait_ge(s_df, g * PAIRS + p)
                        for hh in range(HEADS):
                            for b in range(2):
                                m = 128 if hh + b == 0 else SLOT
                                t0 = PT_ * p + NT * b
                                last = mm(ps_s[SLOT * b:SLOT * b + m, hh // 6, NT * (hh % 6):NT * (hh % 6 + 1)],
                                          q3[0:3 * HD, hh, t0:t0 + m], k3[0:3 * HD, hh, t0:t0 + NT], start=True, stop=True)
                        last.then_inc(p_s, 1)

                def p_(p):
                    if runs(HDS, s):
                        g = gs[HDS]
                        pe.wait_ge(s_p2, g * PAIRS + (p + 1))
                        if p or not isinstance(s, int) or s > HDS:
                            pe.wait_ge(s_p2T, g * PAIRS + p)
                        for half in range(2):
                            for a in range(3):
                                last = nc.tensor.transpose(ps_p[:, half, 128 * a:128 * (a + 1)],
                                                           p2[:, 6 * half + 2 * a:6 * half + 2 * a + 2, :].rearrange("p a b -> p (a b)"),
                                                           ident[:])
                        last.then_inc(p_p, 1)

                def pv(p):
                    if runs(HDS, s):
                        g, gp = gs[HDS], gpar[HDS]
                        if p == 0:
                            pe.wait_ge(s_v2, (g + 1) * 64)
                        pe.wait_ge(s_p2T, g * PAIRS + (p + 1))
                        bank_free(pe, f"pv{p}", s)
                        w = 2 * (HD + 1)
                        for hh in range(HEADS):
                            last = split_product(bank(f"pv{p}")[:, w * hh:w * (hh + 1)].rearrange("p (b e) -> p b e", b=2),
                                                 [p2T[:, part, hh // 2, :] for part in range(2)],
                                                 [v2[:, gp, :, hh % 2, part, p, hh // 2, :] for part in range(2)], True, True)
                        last.then_inc(p_pv, 1)

                def ot(kh):
                    if runs(HDS, s):
                        if kh == 0:
                            pe.wait_ge(s_o2, gs[HDS] * 8 + 8)
                        bank_free(pe, f"ot{kh}", s)
                        for p in range(PAIRS):
                            last = nc.tensor.transpose(bank(f"ot{kh}")[0:DH, 128 * p:128 * (p + 1)],
                                                       o2[:, p, DH * kh:DH * (kh + 1)], ident[:])
                        last.then_inc(p_ot, 1)

                def pr(n):
                    if runs(HDS, s):
                        if n == 0:
                            pe.wait_ge(s_o2T, gs[HDS] * 2 + 2)
                        bank_free(pe, f"pr{n}", s)
                        for p in (2 * n, 2 * n + 1):
                            last = tokens_times(f"pr{n}", p, lambda part, kh: o2T[:, part, kh, PT_ * p:PT_ * (p + 1)],
                                                lambda part, kh: w_pr[:, part, kh, :], D, D * (p % 2))
                        last.then_inc(p_pr, 1)

                s_(0)
                g_(0)
                tok(0)
                g_(1)
                s_(1)
                ga_(0)
                v_(0)
                p_(0)
                ga_(1)
                tok(1)
                v_(1)
                pv(0)
                tok(2)
                sc()
                s_(2)
                tok(3)
                p_(1)
                at()
                tok(4)
                pv(1)
                qk_(0)
                s_(3)
                pt()
                qk_(1)
                p_(2)
                tok(5)
                qk_(2)
                pv(2)
                cv(0)
                tok(6)
                cv(1)
                av(0)
                p_(3)
                av(1)
                tok(7)
                pv(3)
                tok(8)
                tok(9)
                ot(0)
                tok(10)
                ot(1)
                tok(11)
                x2t(0)
                pr(0)
                pr(1)
                x2t(1)
                xt()

            program(pe, step)


def as_shape(src, like, odd=None):
    if odd is not None:
        return src.rearrange("p (h s e) -> p s h e", s=2, e=HD)[:, odd]
    if len(like.shape) == 2:
        return src
    return src.rearrange("p (a c) -> p a c", a=like.shape[1])


_INS = ["x", "L0_tok_W", "L0_tok_b", "L0_attn_Wq", "L0_attn_Wk", "L0_attn_Wv", "L0_ffn_W_qkv", "L0_ffn_b_qkv",
        "L0_ffn_W_gate", "L0_ffn_b_gate", "L0_ffn_A", "L0_ffn_B_lora", "L0_ffn_W_proj", "L0_ffn_b_proj"]


def kernel(**inputs):
    import numpy as np
    import concourse.bacc as bacc
    from concourse.bass_utils import run_bass_kernel_spmd

    nc = bacc.Bacc("TRN2", target_bir_lowering=False, num_devices=1)
    arrays, args = {}, []
    for name in _INS:
        a = np.ascontiguousarray(inputs[name])
        arrays[name] = a
        args.append(nc.dram_tensor(name, a.shape, mybir.dt.from_np(a.dtype), kind="ExternalInput").ap())
    out = nc.dram_tensor("out", (B, NT, D), F32, kind="ExternalOutput").ap()
    scratch = nc.dram_tensor("qk_scratch", (2, 2, 2 * D, TG), F16, kind="Internal").ap()
    audio_tower(nc, *args, out, scratch)
    r = run_bass_kernel_spmd(nc, [arrays], core_ids=[0])
    return r.results[0]["out"]
```

```python
import concourse.bass as bass
from concourse import mybir
from contextlib import ExitStack

F32 = mybir.dt.float32
F16 = mybir.dt.float16
ALU = mybir.AluOpType
ACT = mybir.ActivationFunctionType
AX_X = mybir.AxisListType.X

B, C, T = 128, 90, 750
PATCH = 16
NT = T // PATCH
D = 192
DH = D // 2
HEADS, HD = 12, 16
N_EXP, RANK = 8, 16
NR = N_EXP * RANK
LN_EPS = 1e-5
LORA_SCALE = 2.0

GB = 8
GROUPS = B // GB
TG = GB * NT
PAIRS = GB // 2
PT_ = 2 * NT
HALF_T = TG // 2
TILES = [(0, 128), (128, 128), (256, TG - 256)]
MAIN = 12
XROW = 96
BLOCKS = [(0, 32), (32, 32), (64, C - 64)]
EXTRA = PATCH - MAIN
SLOT = 64
PAD = 128 - PT_

WS = 256.0
QS = 16.0
VS = 16.0
HSCALE = HD ** -0.5

SPLIT, TOK, ATT, MIX, HDS = 0, 1, 2, 3, 4
STEPS = GROUPS + HDS
PEELED = HDS + 2

RING = [("g0", ATT), ("ga0", MIX), ("ga1", MIX), ("g1", ATT), ("v0", ATT), ("pv0", HDS), ("sc", ATT),
        ("v1", ATT), ("at", MIX), ("pv1", HDS), ("qk0", MIX), ("cv0", MIX), ("qk1", MIX), ("qk2", MIX),
        ("pt", ATT), ("pv2", HDS), ("av0", ATT), ("av1", ATT), ("cv1", MIX), ("pv3", HDS), ("ot0", HDS),
        ("ot1", HDS), ("x2t0", ATT), ("pr0", HDS), ("pr1", HDS), ("x2t1", ATT), ("xt0", TOK),
        ("xt1", TOK)]
RING_AT = {name: n % 3 for n, (name, _) in enumerate(RING)}

TOP_LINKS = 18
TOP_SHIFTED = 3


def audio_tower(nc, x, tok_W, tok_b, Wq, Wk, Wv, W_qkv, b_qkv, W_gate, b_gate, A, B_lora,
                W_proj, b_proj, out, scratch):
    with ExitStack() as ctx:
        def sb(name, shape, dt=F32):
            return ctx.enter_context(nc.sbuf_tensor(name, shape, dt))

        def sem(name):
            return ctx.enter_context(nc.semaphore(name))

        ident = sb("ident", [128, 128])
        mask = sb("mask", [PT_, PT_])
        rank_row = sb("rank_row", [PT_, PAIRS, N_EXP])
        minus_half = sb("minus_half", [128, 4])
        eps = sb("eps", [128, 4])
        carrier = sb("carrier", [1, 1])
        w_tok = sb("w_tok", [128, 2, MAIN, D], F16)
        w_m = sb("w_m", [DH, 2, 2, D], F16)
        w_v1 = sb("w_v1", [DH, 2, 2, D], F16)
        w_ga = sb("w_ga", [DH, 2, 2, NR + N_EXP], F16)
        w_qk = sb("w_qk", [DH, 2, 2, 2 * D], F16)
        w_v2 = sb("w_v2", [DH, 2, 2, D], F16)
        w_lora = sb("w_lora", [NR, 2, 3 * D], F16)
        w_pr = sb("w_pr", [DH, 2, 2, D], F16)
        b_tok_bc = sb("b_tok_bc", [128, D])
        b_v = sb("b_v", [DH, 2])
        b_pr_bc = sb("b_pr_bc", [PT_, D])
        b_gate_bc = sb("b_gate_bc", [PT_, N_EXP])
        b_qk = sb("b_qk", [128, 3])
        raw = sb("raw", [C, 2, GB // 2, NT * PATCH])
        xs = sb("xs", [128, 2, 2, MAIN, TG], F16)
        xe = sb("xe", [C, 2, EXTRA, TG], F16)
        h = sb("h", [128, 3, D])
        st1 = sb("st1", [128, 3, 6])
        mv1 = sb("mv1", [128, 3, 2])
        ve1 = sb("ve1", [128, 3])
        rs1 = sb("rs1", [128, 3])
        xn = sb("xn", [128, 3, D])
        xnT = sb("xnT", [DH, 2, 2, 2, TG + PAD], F16)
        hp = sb("hp", [PT_, 2, PAIRS, D])
        gT = sb("gT", [DH, 2, 2, TG], F16)
        v1 = sb("v1", [PT_, PAIRS, D])
        sm = sb("sm", [PT_, PAIRS, PT_])
        m1 = sb("m1", [PT_, PAIRS])
        nm1 = sb("nm1", [PT_, PAIRS])
        p1 = sb("p1", [PT_, PAIRS, PT_])
        l1 = sb("l1", [PT_, PAIRS])
        rl1 = sb("rl1", [PT_, PAIRS])
        p1T = sb("p1T", [PT_, PAIRS, PT_])
        h2 = sb("h2", [PT_, 2, PAIRS, D])
        st2 = sb("st2", [PT_, PAIRS, 6])
        mv2 = sb("mv2", [PT_, PAIRS, 2])
        ve2 = sb("ve2", [PT_, PAIRS])
        rs2 = sb("rs2", [PT_, PAIRS])
        xn2 = sb("xn2", [PT_, PAIRS, D])
        x2T = sb("x2T", [DH, 2, 2, 2, TG], F16)
        ga = sb("ga", [PT_, PAIRS, NR + N_EXP])
        lg = sb("lg", [PT_, PAIRS, N_EXP])
        lg2 = sb("lg2", [PT_, PAIRS, N_EXP])
        key = sb("key", [PT_, 2, PAIRS, N_EXP])
        hot = sb("hot", [PT_, 2, PAIRS, N_EXP])
        top = sb("top", [PT_, 2, PAIRS])
        best = sb("best", [PT_, 2, PAIRS])
        lgm = sb("lgm", [PT_, PAIRS, N_EXP])
        pe_x = sb("pe_x", [PT_, PAIRS, N_EXP])
        pe_s = sb("pe_s", [PT_, PAIRS])
        pe_r = sb("pe_r", [PT_, PAIRS])
        both = sb("both", [PT_, PAIRS, N_EXP])
        disp0 = sb("disp0", [PT_, PAIRS, N_EXP])
        disp = sb("disp", [PT_, PAIRS, N_EXP])
        ad = sb("ad", [PT_, PAIRS, NR])
        adT = sb("adT", [NR, 2, TG], F16)
        qk = sb("qk", [128, 2, 3, TG], F16)
        v2s = sb("v2s", [PT_, 2, 2, 2, PAIRS // 2, HEADS // 2, HD + 1], F16)
        h2b = sb("h2b", [PT_, 2, PAIRS, D])
        q3 = sb("q3", [128, HEADS, TG + PAD], F16)
        k3 = sb("k3", [128, HEADS, TG], F16)
        v2_flat = sb("v2", [128, 2 * 2 * 2 * 2 * PAIRS * HEADS // 2 * (HD + 1)], F16)
        v2 = v2_flat[:].rearrange("p (a b c d e f g) -> p a b c d e f g", a=2, b=2, c=2, d=2, e=PAIRS, f=HEADS // 2)
        mx = sb("mx", [128, HEADS])
        df = sb("df", [128, HEADS, NT])
        p2 = sb("p2", [128, HEADS, SLOT])
        p2T = sb("p2T", [128, 2, HEADS // 2, 128], F16)
        rc = sb("rc", [128, HEADS])
        o2 = sb("o2", [128, PAIRS, D])
        o2T = sb("o2T", [DH, 2, 2, TG], F16)

        v2_room = v2_flat[:].bitcast(F32)
        st_tok = v2_room[0:DH, 0:2 * C * PATCH]
        q_room = q3[:].rearrange("p a b -> p (a b)").bitcast(F32)
        k_room = k3[:].rearrange("p a b -> p (a b)").bitcast(F32)
        st_q = q_room[0:DH, 0:2 * D]
        st_k = q_room[0:DH, 2 * D:4 * D]
        st_v = q_room[0:DH, 4 * D:6 * D]
        st_pr = q_room[0:DH, 6 * D:8 * D]
        st_a = q_room[0:NR, 8 * D:9 * D]
        st_g = q_room[0:N_EXP, 9 * D:10 * D]
        st_qkv = k_room[0:DH, 0:6 * D]
        st_b = k_room[0:DH, 6 * D:6 * D + 6 * NR]
        qk_T = p2T[0:DH].rearrange("p a b c -> p (a b c)").bitcast(F32)
        bias_v = o2T[:, :, :, 0:PT_]
        ps_tok = ctx.enter_context(nc.psum_tensor("ps_tok", [128, 512], F32))
        ps_s = ctx.enter_context(nc.psum_tensor("ps_s", [128, 2, 512], F32))
        ps_p = ctx.enter_context(nc.psum_tensor("ps_p", [128, 2, 512], F32))
        ps_r = ctx.enter_context(nc.psum_tensor("ps_r", [128, 3, 512], F32))

        s_wt = sem("tok_W_loaded")
        s_w = sem("weights_loaded")
        s_ident = sem("ident_ready")
        s_zero = sem("pads_cleared")
        s_maskf = sem("mask_ready")
        s_ut = sem("unit_transposed")
        s_uh = sem("unit_high_ready")
        s_ul = sem("unit_low_ready")
        s_wd = sem("direct_weights")
        s_wz = sem("rows_cleared")
        s_bv = sem("value_bias_links")
        p_bv = sem("value_bias_projected")
        s_x = [sem("x_loaded_0"), sem("x_loaded_1")]
        s_xrow = sem("extra_rows_moved")
        s_hp = sem("h_in_pairs")
        s_scw = sem("qk_in_scratch")
        s_qk3 = sem("qk_stacked")
        s_v2 = sem("v2_placed")
        s_out = [sem("out_stored_even"), sem("out_stored_odd")]
        s_hi = sem("x_high_ready")
        s_lo = sem("x_low_ready")
        p_tok = sem("tok_done")
        p_xt = sem("xt_done")
        p_g = sem("g_done")
        p_v = sem("v_done")
        p_sc = sem("scores1_done")
        p_pt = sem("p1_transposed")
        p_av = sem("attn1_done")
        p_x2t = sem("x2t_done")
        p_ga = sem("ga_done")
        p_at = sem("ad_transposed")
        p_qk = sem("qk_done")
        p_cv = sem("v2_done")
        p_s = sem("scores2_done")
        p_p = sem("p2_transposed")
        p_pv = sem("attn2_done")
        p_ot = sem("o2_transposed")
        p_pr = sem("proj_done")
        s_h = sem("h_ready")
        s_ln1 = sem("ln1_links")
        s_var1 = sem("var1_ready")
        s_rs1 = sem("rstd1_ready")
        s_ve1 = sem("var1_eps_ready")
        s_xn = sem("xn_ready")
        s_xnh = sem("xnT_high_ready")
        s_xnT = sem("xnT_ready")
        s_gh = sem("gT_high_ready")
        s_gT = sem("gT_ready")
        s_v1 = sem("v1_ready")
        s_sm = sem("scores1_masked")
        s_m1 = sem("max1_links")
        s_p1 = sem("p1_ready")
        s_p1T = sem("p1T_ready")
        s_rl1 = sem("sum1_inverted")
        s_h2 = sem("h2_ready")
        s_ln2 = sem("ln2_links")
        s_ve2 = sem("var2_eps_ready")
        s_rs2 = sem("rstd2_ready")
        s_xn2 = sem("xn2_ready")
        s_x2h = sem("x2T_high_ready")
        s_x2T = sem("x2T_ready")
        s_ga = sem("ga_ready")
        s_top = sem("top2_links")
        s_pex = sem("router_exp_ready")
        s_ad = sem("ad_ready")
        s_adh = sem("adT_high_ready")
        s_adT = sem("adT_ready")
        s_qkh = sem("qk_high_ready")
        s_qkl = sem("qk_low_ready")
        s_v2h = sem("v2_high_ready")
        s_v2s = sem("v2_evacuated")
        s_h2b = sem("h2b_ready")
        s_mx = sem("max2_ready")
        s_df = sem("scores2_shifted")
        s_p2 = sem("p2_ready")
        s_p2h = sem("p2T_high_ready")
        s_p2T = sem("p2T_ready")
        s_rc = sem("sum2_inverted")
        s_o2 = sem("o2_ready")
        s_oh = sem("o2T_high_ready")
        s_o2T = sem("o2T_ready")
        s_fin = sem("out_ready")

        FREED = {"g0": (s_gT, 2, 1), "g1": (s_gT, 2, 2), "v0": (s_v1, 2, 1), "v1": (s_v1, 2, 2),
                 "ga0": (s_ga, 2, 1), "ga1": (s_ga, 2, 2), "sc": (s_sm, 1, 1), "at": (s_adT, 1, 1),
                 "pt": (s_p1T, 1, 1), "av0": (s_h2, 4, 2), "av1": (s_h2, 4, 4),
                 "qk0": (s_qkl, 3, 1), "qk1": (s_qkl, 3, 2), "qk2": (s_qkl, 3, 3),
                 "cv0": (s_v2s, 2, 1), "cv1": (s_v2s, 2, 2),
                 "pv0": (s_o2, 8, 2), "pv1": (s_o2, 8, 4), "pv2": (s_o2, 8, 6), "pv3": (s_o2, 8, 8),
                 "ot0": (s_o2T, 2, 1), "ot1": (s_o2T, 2, 2), "pr0": (s_fin, 2, 1), "pr1": (s_fin, 2, 2),
                 "x2t0": (s_x2T, 2, 1), "x2t1": (s_x2T, 2, 2), "xt0": (s_xnT, 2, 1), "xt1": (s_xnT, 2, 2)}

        def runs(stage_lag, s):
            return not isinstance(s, int) or 0 <= s - stage_lag < GROUPS

        def bank(name):
            return ps_r[:, RING_AT[name], :]

        def bank_free(pe, name, s):
            at = [n for n, _ in RING].index(name)
            for back in range(1, 200):
                n = at - back
                steps_back, n = -(n // len(RING)), n % len(RING)
                prev, lag = RING[n]
                if RING_AT[prev] != RING_AT[name]:
                    continue
                if isinstance(s, int):
                    if s - steps_back < 0:
                        return
                    if not runs(lag, s - steps_back):
                        continue
                freed, per, place = FREED[prev]
                pe.wait_ge(freed, (s - lag) * per + (place - steps_back * per))
                return

        x_v = x.rearrange("b c t -> c b t")
        out_v = out.rearrange("b n d -> (b n) d").rearrange("(q r) d -> r q d", r=PT_)
        w_in = scratch.rearrange("a b (t p) n -> a p b t n", p=128)
        w_out = scratch.rearrange("a b (h d) n -> a b d h n", d=HD)


        UNITS = []

        def transposes_of(blocks):
            return [("t", at, src) for at, src in blocks]

        def heads_of(ap):
            return ap.rearrange("p (h e) -> p h e", e=HD)

        tokv = st_tok.rearrange("p (a c k) -> p a c k", a=2, k=PATCH)
        for j in range(0, MAIN, 2):
            blocks = [(D * jj + DH * e, tokv[:, e, :, j + jj]) for jj in range(2) for e in range(2)]
            UNITS.append((transposes_of(blocks), C, 2 * D, w_tok[0:C, 0, j:j + 2, :], w_tok[0:C, 1, j:j + 2, :], WS))
        for blk, (c0, n) in enumerate(BLOCKS):
            for q in range(0, EXTRA, 2):
                blocks = [(D * qq + DH * e, tokv[:, e, c0:c0 + n, MAIN + q + qq]) for qq in range(2) for e in range(2)]
                j = EXTRA * blk + q
                UNITS.append((transposes_of(blocks), n, 2 * D, w_tok[XROW:XROW + n, 0, j:j + 2, :],
                              w_tok[XROW:XROW + n, 1, j:j + 2, :], WS))
        TOK_UNITS = len(UNITS)
        for n, st in enumerate((st_q, st_k)):
            stv = st.rearrange("p (a c) -> p a c", a=2)
            blocks = [(D * hh + DH * ih, stv[:, ih, DH * hh:DH * hh + DH]) for hh in range(2) for ih in range(2)]
            dst = qk_T[:, 2 * D * n:2 * D * n + 2 * D]
            UNITS.append((transposes_of(blocks), DH, 2 * D, dst[:, 0:D], dst[:, D:2 * D], None))
        M_FROM = len(UNITS)
        UNITS.append(([("m", D * ih, ih) for ih in range(2)], DH, 2 * D, w_m[:, 0, :, :], w_m[:, 1, :, :], WS))
        for kh in range(2):
            qkvv = st_qkv.rearrange("p (a c) -> p a c", a=6)[:, :, DH * kh:DH * kh + DH]
            UNITS.append((transposes_of([(DH * a, qkvv[:, a, :]) for a in range(4)]), DH, 2 * D,
                          w_qk[:, 0, kh, :], w_qk[:, 1, kh, :], QS))
            for odd in range(2):
                UNITS.append((transposes_of([(DH * a, qkvv[:, 4 + a, :]) for a in range(2)]), DH, D,
                              *(heads_of(w_v2[:, part, kh, DH * odd:DH * (odd + 1)]) for part in range(2)), WS, odd))
            UNITS.append((transposes_of([(0, st_a[:, DH * kh:DH * kh + DH]), (NR, st_g[:, DH * kh:DH * kh + DH])]),
                          DH, NR + N_EXP, w_ga[:, 0, kh, :], w_ga[:, 1, kh, :], WS))
            prv = st_pr.rearrange("p (a c) -> p a c", a=2)[:, :, DH * kh:DH * kh + DH]
            UNITS.append((transposes_of([(DH * a, prv[:, a, :]) for a in range(2)]), DH, D,
                          w_pr[:, 0, kh, :], w_pr[:, 1, kh, :], WS))
        bv = st_b.rearrange("p (a c) -> p a c", a=6)
        UNITS.append((transposes_of([(DH * a, bv[:, a, :]) for a in range(4)]), NR, 2 * D,
                      w_lora[:, 0, 0:2 * D], w_lora[:, 1, 0:2 * D], QS))
        for odd in range(2):
            cols = slice(2 * D + DH * odd, 2 * D + DH * (odd + 1))
            UNITS.append((transposes_of([(DH * a, bv[:, 4 + a, :]) for a in range(2)]), NR, D,
                          *(heads_of(w_lora[:, part, cols]) for part in range(2)), WS, odd))
        N_LOADS = 21
        HP_DMAS = 6

        def v2_split(n, part):
            return (v2s[:, part, n, :, :, :, 0:HD].rearrange("p s a h e -> p (s a h) e"), heads_of(bank(f"cv{n}")[0:PT_, 0:2 * D]))

        def unit_bank(n, rows, cols):
            return ps_r[0:rows, n % 3, 0:cols]

        block = ctx.enter_context(nc.Block())

        def program(engine, step):
            for s in range(PEELED):
                step(s, s % 2)
            with engine.Fori(PEELED // 2, GROUPS // 2 - 1) as i:
                step(i * 2, 0)
                step(i * 2 + 1, 1)
            for s in range(GROUPS - 2, STEPS):
                step(s, s % 2)

        @block.sync
        def _(sp):
            def load(dst, src):
                sp.dma_start(dst, src).then_inc(s_w, 16)

            def clips(g, half):
                b0 = g * GB + half * (GB // 2)
                return x_v[:, bass.ds(b0 if isinstance(g, int) else sp.snap(b0), GB // 2), 0:NT * PATCH]

            def count(value):
                return value if isinstance(value, int) else sp.snap(value)

            def load_x(src, half):
                sp.dma_start(raw[:, half, :, :], src).then_inc(s_x[half], 16)

            sp.dma_start(st_tok.rearrange("p (a f) -> p a f", a=2),
                         tok_W.rearrange("(a p) f -> p a f", p=DH)).then_inc(s_wt, 16)
            load_x(clips(0, 0), 0)
            load_x(clips(0, 1), 1)
            for st, w in ((st_q, Wq), (st_k, Wk), (st_v, Wv), (st_pr, W_proj)):
                load(st.rearrange("p (a c) -> p a c", a=2), w.rearrange("(a p) c -> p a c", p=DH))
            load(st_qkv.rearrange("p (a c) -> p a c", a=6), W_qkv.rearrange("(a p) c -> p a c", p=DH))
            load(st_a, A.rearrange("n r d -> (n r) d"))
            load(st_g, W_gate)
            for a in range(6):
                load(st_b[:, NR * a:NR * (a + 1)].rearrange("p (n r) -> p n r", n=N_EXP),
                     B_lora[:, DH * a:DH * (a + 1), :].rearrange("n p r -> p n r"))
            row = lambda v, rows: v.rearrange("(a d) -> a d", a=1).broadcast_to([rows, v.shape[0]])
            load(b_tok_bc[:], row(tok_b, 128))
            for kh in range(2):
                load(b_v[:, kh:kh + 1], b_qkv[2 * D + DH * kh:2 * D + DH * (kh + 1)].rearrange("(p a) -> p a", a=1))
            load(b_pr_bc[:], row(b_proj, PT_))
            load(b_gate_bc[:], row(b_gate, PT_))
            for t in range(3):
                load(b_qk[:, t:t + 1], b_qkv[128 * t:128 * (t + 1)].rearrange("(p a) -> p a", a=1))

            def step(s, par):
                if runs(SPLIT, s):
                    sp.wait_ge(s_lo, s * 16 + 4)
                    for blk, (c0, n) in enumerate(BLOCKS):
                        sp.dma_start(xs[XROW:XROW + n, par, :, EXTRA * blk:EXTRA * (blk + 1), :],
                                     xe[c0:c0 + n, :, :, :]).then_inc(s_xrow, 16)
                if runs(SPLIT, s) and (not isinstance(s, int) or s + 1 < GROUPS):
                    src = clips(s + 1, 0)
                    sp.wait_ge(s_lo, s * 16 + 10)
                    load_x(src, 0)
                if runs(MIX, s):
                    g = s - MIX
                    gp = (par - MIX) % 2
                    if isinstance(s, int) and s == MIX:
                        sp.wait_ge(s_wz, 4)
                    sp.wait_ge(s_qkl, g * 3 + 3)
                    for part in range(2):
                        sp.dma_start(w_in[gp, :, part, :, :], qk[:, part, :, :]).then_inc(s_scw, 16)
                    written, read = count(g * 32 + 32), None
                    if not isinstance(s, int) or s - HDS >= 0:
                        read = count((s - HDS) * PAIRS + PAIRS)
                    sp.wait_ge(s_scw, written)
                    if read is not None:
                        sp.wait_ge(p_s, read)
                    for n, (qp, kp) in enumerate(((0, 0), (1, 0), (0, 1))):
                        sp.dma_start(q3[HD * n:HD * (n + 1), :, 0:TG], w_out[gp, qp, :, 0:HEADS, :]).then_inc(s_qk3, 16)
                        sp.dma_start(k3[HD * n:HD * (n + 1), :, :], w_out[gp, kp, :, HEADS:2 * HEADS, :]).then_inc(s_qk3, 16)
                    sp.wait_ge(s_v2s, g * 2 + 2)
                    for b in range(2):
                        for odd in range(2):
                            sp.dma_start(v2[SLOT * odd:SLOT * odd + NT, gp, b, odd].rearrange("p l (n a) h e -> p (l n) (a h e)", n=2),
                                         v2s[NT * b:NT * b + NT, :, :, odd].rearrange("p l n a h e -> p (l n) (a h e)")).then_inc(s_v2, 16)
                if runs(SPLIT, s) and (not isinstance(s, int) or s + 1 < GROUPS):
                    src = clips(s + 1, 1)
                    sp.wait_ge(s_lo, s * 16 + 16)
                    load_x(src, 1)
                if runs(TOK, s):
                    g = s - TOK
                    gp = (par - TOK) % 2
                    sp.wait_ge(s_h, g * 3 + 3)
                    for p in range(PAIRS):
                        at = p * PT_
                        while at < (p + 1) * PT_:
                            t = min(at // 128, 2)
                            n = min((t + 1) * 128, (p + 1) * PT_) - at
                            sp.dma_start(hp[at - p * PT_:at - p * PT_ + n, gp, p, :],
                                         h[at - 128 * t:at - 128 * t + n, t, :]).then_inc(s_hp, 16)
                            at += n
                if runs(HDS, s):
                    g = s - HDS
                    first = g * PAIRS if isinstance(g, int) else sp.snap(g * PAIRS)
                    sp.wait_ge(s_fin, g * 2 + 2)
                    sp.dma_start(out_v[:, bass.ds(first, PAIRS), :],
                                 h2b[:, (par - HDS) % 2, :, :]).then_inc(s_out[(par - HDS) % 2], 16)

            program(sp, step)
            for parity in range(2):
                sp.wait_ge(s_out[parity], GROUPS // 2 * 16)

        @block.gpsimd
        def _(pool):
            nc.gpsimd.memset(ident[:], 0.0).then_inc(s_zero, 1)
            pool.wait_ge(s_zero, 1)
            nc.gpsimd.affine_select(out=ident[:], in_=ident[:], compare_op=ALU.not_equal, fill=1.0, base=0,
                                    pattern=[[-1, 128]], channel_multiplier=1).then_inc(s_ident, 1)
            nc.gpsimd.memset(mask[:], 0.0).then_inc(s_zero, 1)
            pool.wait_ge(s_zero, 2)
            nc.gpsimd.affine_select(out=mask[:], in_=mask[:], compare_op=ALU.is_ge, fill=-3e38, base=0,
                                    pattern=[[-1, PT_]], channel_multiplier=1).then_inc(s_zero, 1)
            pool.wait_ge(s_zero, 3)
            nc.gpsimd.affine_select(out=mask[:, 0:NT], in_=mask[:, 0:NT], compare_op=ALU.is_ge, fill=-3e38,
                                    base=NT - 1, pattern=[[0, NT]], channel_multiplier=-1).then_inc(s_maskf, 1)
            nc.gpsimd.memset(minus_half[:], -0.5).then_inc(s_maskf, 1)
            nc.gpsimd.memset(eps[:], LN_EPS).then_inc(s_maskf, 1)
            for e in range(N_EXP):
                nc.gpsimd.memset(rank_row[:, :, e:e + 1], float(N_EXP - e)).then_inc(s_maskf, 1)
            nc.gpsimd.memset(xnT[:, :, :, :, TG:TG + PAD], 0.0).then_inc(s_maskf, 1)
            nc.gpsimd.memset(p2[:, :, NT:SLOT], 0.0).then_inc(s_maskf, 1)
            nc.gpsimd.memset(v2s[:, 0, :, :, :, :, HD:HD + 1], 1.0).then_inc(s_maskf, 1)
            nc.gpsimd.memset(v2s[:, 1, :, :, :, :, HD:HD + 1], 0.0).then_inc(s_maskf, 1)
            pool.wait_ge(s_maskf, 15)
            nc.gpsimd.memset(f32_of(xs[64:128, 1]), 0.0).then_inc(s_maskf, 1)
            pool.wait_ge(s_maskf, 16)

            def low_of_x(s, par, n):
                raw_v = raw[:].rearrange("p f b (n k) -> p f (b n) k", k=PATCH)
                if n < 4:
                    half, ph = n // 2, MAIN + 2 * (n % 2)
                    hi = xe[:, 0, ph - MAIN:ph - MAIN + 2, HALF_T * half:HALF_T * (half + 1)]
                    lo = xe[:, 1, ph - MAIN:ph - MAIN + 2, HALF_T * half:HALF_T * (half + 1)]
                    need = half + 1
                else:
                    half, ph = (n - 4) // 6, 2 * ((n - 4) % 6)
                    hi = xs[0:C, par, 0, ph:ph + 2, HALF_T * half:HALF_T * (half + 1)]
                    lo = xs[0:C, par, 1, ph:ph + 2, HALF_T * half:HALF_T * (half + 1)]
                    need = 2 + 3 * half + (ph // 4) + 1
                pool.wait_ge(s_hi, s * 8 + need)
                nc.gpsimd.tensor_tensor(lo, raw_v[:, half, :, ph:ph + 2].rearrange("p t k -> p k t"),
                                        hi, ALU.subtract).then_inc(s_lo, 1)

            def rstd(ready, count, src, dst, ve, ve_sem, done, n_done):
                rows, cols = ve.shape[0], ve.shape[1]
                pool.wait_ge(ready, count)
                nc.gpsimd.tensor_tensor(ve, src, eps[0:rows, 0:cols], ALU.add).then_inc(ve_sem, 1)
                pool.wait_ge(ve_sem, n_done)
                nc.gpsimd.tensor_tensor(dst, ve, minus_half[0:rows, 0:cols], ALU.pow).then_inc(done, 1)
                pool.wait_ge(done, n_done)

            def step(s, par):
                given, of_others = [0], [False]

                def lows_done():
                    if runs(SPLIT, s) and given[0] and not of_others[0]:
                        pool.wait_ge(s_lo, s * 16 + given[0])
                    of_others[0] = True

                def low(n):
                    if runs(SPLIT, s):
                        low_of_x(s, par, n)
                    given[0] = n + 1
                    of_others[0] = False

                def ad_():
                    lows_done()
                    if runs(MIX, s):
                        g = s - MIX
                        pool.wait_ge(s_top, g * TOP_LINKS + TOP_LINKS)
                        nc.gpsimd.tensor_tensor(ad[:].rearrange("p a (n r) -> p a n r", n=N_EXP),
                                                ga[:, :, 0:NR].rearrange("p a (n r) -> p a n r", n=N_EXP),
                                                disp[:].unsqueeze(3).to_broadcast([PT_, PAIRS, N_EXP, RANK]),
                                                ALU.mult).then_inc(s_ad, 1)
                        pool.wait_ge(s_ad, g + 1)

                def ln1(t):
                    lows_done()
                    if runs(TOK, s):
                        g, m = s - TOK, TILES[t][1]
                        rstd(s_var1, g * 3 + (t + 1), mv1[0:m, t, 1:2], rs1[0:m, t:t + 1],
                             ve1[0:m, t:t + 1], s_ve1, s_rs1, g * 3 + (t + 1))

                def ln2():
                    lows_done()
                    if runs(ATT, s):
                        g = s - ATT
                        rstd(s_ln2, g * 5 + 5, mv2[:, :, 1], rs2[:, :], ve2[:, :], s_ve2, s_rs2, g + 1)

                def h2b_():
                    lows_done()
                    if runs(MIX, s):
                        g = s - MIX
                        gp = (par - MIX) % 2
                        pool.wait_ge(s_xn2, g * PAIRS + PAIRS)
                        if not isinstance(s, int) or g >= 2:
                            pool.wait_ge(s_out[gp], (g - gp) * 8)
                        nc.gpsimd.tensor_tensor(h2b[:, gp, :, :], h2[:, gp, :, :],
                                                b_pr_bc[:].unsqueeze(1).to_broadcast([PT_, PAIRS, D]),
                                                ALU.add).then_inc(s_h2b, 1)
                        pool.wait_ge(s_h2b, g + 1)

                low(0)
                ad_()
                ln1(0)
                low(1)
                h2b_()
                low(2)
                low(3)
                low(4)
                low(5)
                low(6)
                low(7)
                low(8)
                low(9)
                low(10)
                ln1(1)
                low(11)
                ln2()
                low(12)
                low(13)
                low(14)
                ln1(2)
                low(15)

            program(pool, step)

        @block.scalar
        def _(act):
            def copy(out_, in_, scale=1.0):
                return nc.scalar.activation(out_, in_, ACT.Copy, scale=scale)

            def high_of_x(s, par, n):
                raw_v = raw[:].rearrange("p f b (n k) -> p f (b n) k", k=PATCH)
                half = n if n < 2 else (n - 2) // 3
                if n < 2:
                    ph = MAIN
                    hi = xe[:, 0, :, HALF_T * half:HALF_T * (half + 1)]
                    if not isinstance(s, int) or s > 0:
                        if n == 0:
                            act.wait_ge(s_xrow, s * 48)
                else:
                    ph = 4 * ((n - 2) % 3)
                    hi = xs[0:C, par, 0, ph:ph + 4, HALF_T * half:HALF_T * (half + 1)]
                act.wait_ge(s_x[half], s * 16 + 16)
                copy(hi, raw_v[:, half, :, ph:ph + 4].rearrange("p t k -> p k t")).then_inc(s_hi, 1)

            act.wait_ge(s_wz, 2)
            for n, (_, rows, cols, hi, lo, scale, *odd) in enumerate(UNITS):
                if n % 2 == 0 and n // 2 < 8:
                    high_of_x(0, 0, n // 2)
                act.wait_ge(s_ut, n + 1)
                src = unit_bank(n, rows, cols)
                if scale is None:
                    copy(hi, src[:, 0:D]).then_inc(s_uh, 1)
                else:
                    copy(hi, as_shape(src, hi, *odd), scale).then_inc(s_uh, 1)
            act.wait_ge(s_w, 16 * N_LOADS)
            copy(w_v1[:, 0, :, :], st_v.rearrange("p (a c) -> p a c", a=2), WS).then_inc(s_wd, 1)

            def step(s, par):
                gs = {lag: s - lag for lag in range(5)}
                gpar = {lag: (par - lag) % 2 for lag in range(5)}

                def exp2(p):
                    if runs(HDS, s):
                        act.wait_ge(s_df, gs[HDS] * PAIRS + (p + 1))
                        if p:
                            act.wait_ge(p_p, gs[HDS] * PAIRS + p)
                        nc.scalar.activation(p2[:, :, 0:NT], df[:], ACT.Exp, scale=HSCALE / (QS * QS)).then_inc(s_p2, 1)

                def p2t(p):
                    if runs(HDS, s):
                        act.wait_ge(p_p, gs[HDS] * PAIRS + (p + 1))
                        if p:
                            act.wait_ge(p_pv, gs[HDS] * PAIRS + p)
                        copy(p2T[:, 0].rearrange("p (a b) c -> p a (b c)", a=2), ps_p[:, :, 0:3 * 128]).then_inc(s_p2h, 1)

                def high(n):
                    if runs(SPLIT, s) and not (isinstance(s, int) and s == 0):
                        high_of_x(s, par, n)

                def g_high(jh):
                    if runs(ATT, s):
                        act.wait_ge(p_g, gs[ATT] * 2 + (jh + 1))
                        copy(gT[:, 0, jh, :], bank(f"g{jh}")[0:DH, 0:TG], 1 / WS).then_inc(s_gh, 1)

                def ga_copy(n):
                    if runs(MIX, s):
                        act.wait_ge(p_ga, gs[MIX] * 2 + (n + 1))
                        copy(ga[:, 2 * n:2 * n + 2, :],
                             bank(f"ga{n}")[0:PT_, 0:2 * (NR + N_EXP)].rearrange("p (a c) -> p a c", a=2), 1 / WS).then_inc(s_ga, 1)

                def v_copy(n):
                    if runs(ATT, s):
                        act.wait_ge(p_v, gs[ATT] * 2 + (n + 1))
                        copy(v1[:, 2 * n:2 * n + 2, :],
                             bank(f"v{n}")[0:PT_, 0:2 * D].rearrange("p (a c) -> p a c", a=2), 1 / WS).then_inc(s_v1, 1)

                def router_exp():
                    if runs(MIX, s):
                        act.wait_ge(s_top, gs[MIX] * TOP_LINKS + TOP_SHIFTED)
                        nc.scalar.activation(pe_x[:], lgm[:], ACT.Exp).then_inc(s_pex, 1)

                def exp1():
                    if runs(ATT, s):
                        for p in range(PAIRS):
                            act.wait_ge(s_m1, gs[ATT] * 2 + 2)
                            nc.scalar.activation(p1[:, p, :], sm[:, p, :], ACT.Exp, bias=nm1[:, p:p + 1],
                                                 accum_out=l1[:, p:p + 1]).then_inc(s_p1, 1)

                def ad_high():
                    if runs(MIX, s):
                        act.wait_ge(p_at, gs[MIX] + 1)
                        copy(adT[:, 0, :], bank("at")[0:NR, 0:TG]).then_inc(s_adh, 1)

                def qk_high(t):
                    if runs(MIX, s):
                        act.wait_ge(p_qk, gs[MIX] * 3 + (t + 1))
                        nc.scalar.activation(qk[:, 0, t, :], bank(f"qk{t}")[:, 0:TG], ACT.Identity,
                                             bias=b_qk[:, t:t + 1]).then_inc(s_qkh, 1)

                def p1t():
                    if runs(ATT, s):
                        act.wait_ge(p_pt, gs[ATT] + 1)
                        copy(p1T[:], bank("pt")[0:PT_, 0:PAIRS * PT_].rearrange("p (a c) -> p a c", a=PAIRS)).then_inc(s_p1T, 1)

                def cv_high(n):
                    if runs(MIX, s):
                        act.wait_ge(p_cv, gs[MIX] * 2 + (n + 1))
                        copy(*v2_split(n, 0), VS / WS).then_inc(s_v2h, 1)

                def o_high(kh):
                    if runs(HDS, s):
                        act.wait_ge(p_ot, gs[HDS] * 2 + (kh + 1))
                        copy(o2T[:, 0, kh, :].rearrange("p (a t) -> p a t", t=NT),
                             bank(f"ot{kh}")[0:DH, :].rearrange("p (a t) -> p a t", t=SLOT)[:, :, 0:NT]).then_inc(s_oh, 1)

                def x2_high(kh):
                    if runs(ATT, s):
                        act.wait_ge(p_x2t, gs[ATT] * 2 + (kh + 1))
                        copy(x2T[:, gpar[ATT], 0, kh, :], bank(f"x2t{kh}")[0:DH, 0:TG]).then_inc(s_x2h, 1)

                def xn_high(kh):
                    if runs(TOK, s):
                        act.wait_ge(p_xt, gs[TOK] * 2 + (kh + 1))
                        copy(xnT[:, gpar[TOK], 0, kh, 0:TG], bank(f"xt{kh}")[0:DH, 0:TG]).then_inc(s_xnh, 1)

                exp2(0)
                g_high(0)
                ga_copy(0)
                high(0)
                ga_copy(1)
                exp2(1)
                p2t(0)
                router_exp()
                high(1)
                g_high(1)
                high(2)
                v_copy(0)
                p2t(1)
                ad_high()
                v_copy(1)
                exp1()
                high(3)
                cv_high(0)
                qk_high(0)
                exp2(2)
                high(4)
                p2t(2)
                qk_high(1)
                qk_high(2)
                high(5)
                p1t()
                exp2(3)
                high(6)
                p2t(3)
                cv_high(1)
                high(7)
                o_high(0)
                o_high(1)
                x2_high(0)
                x2_high(1)
                xn_high(0)
                xn_high(1)

            program(act, step)

        @block.vector
        def _(dve):
            nc.vector.memset(f32_of(w_tok[64:128]), 0.0).then_inc(s_wz, 1)
            nc.vector.memset(f32_of(xs[64:128, 0]), 0.0).then_inc(s_wz, 1)
            for n, (_, rows, cols, hi, lo, scale, *odd) in enumerate(UNITS):
                if n == TOK_UNITS:
                    dve.wait_ge(s_w, 16 * N_LOADS)
                    nc.vector.tensor_scalar(b_qk[:], b_qk[:], QS, None, ALU.mult).then_inc(s_bv, 1)
                    nc.vector.tensor_scalar(bias_v[:, 0], b_v[:].unsqueeze(2).to_broadcast([DH, 2, PT_]), QS, None,
                                            ALU.mult).then_inc(s_bv, 1)
                    dve.wait_ge(s_bv, 2)
                    nc.vector.scalar_tensor_tensor(out=bias_v[:, 1], in0=b_v[:].unsqueeze(2).to_broadcast([DH, 2, PT_]), scalar=QS,
                                                   in1=bias_v[:, 0], op0=ALU.mult, op1=ALU.subtract).then_inc(s_bv, 1)
                dve.wait_ge(s_uh, n + 1)
                src = unit_bank(n, rows, cols)
                if scale is None:
                    nc.vector.tensor_copy(lo, src[:, D:2 * D]).then_inc(s_ul, 1)
                else:
                    nc.vector.scalar_tensor_tensor(out=lo, in0=as_shape(src, hi, *odd), scalar=scale, in1=hi,
                                                   op0=ALU.mult, op1=ALU.subtract).then_inc(s_ul, 1)
            dve.wait_ge(s_wd, 1)
            nc.vector.scalar_tensor_tensor(out=w_v1[:, 1, :, :], in0=st_v.rearrange("p (a c) -> p a c", a=2), scalar=WS,
                                           in1=w_v1[:, 0, :, :], op0=ALU.mult, op1=ALU.subtract).then_inc(s_wd, 1)
            dve.wait_ge(s_wd, 2)
            dve.wait_ge(p_bv, 1)
            nc.vector.scalar_tensor_tensor(out=b_pr_bc[:], in0=ps_s[0:PT_, 0, 0:D], scalar=1 / (WS * QS),
                                           in1=b_pr_bc[:], op0=ALU.mult, op1=ALU.add).then_inc(s_bv, 1)
            nc.vector.memset(v2_room, 0.0).then_inc(s_wz, 1)
            nc.vector.memset(q3[0:3 * HD, :, TG:], 0.0).then_inc(s_wz, 1)

            def step(s, par):
                gs = {lag: s - lag for lag in range(5)}
                gpar = {lag: (par - lag) % 2 for lag in range(5)}

                def low(out_, src, hi, scale, ready, count, done):
                    dve.wait_ge(ready, count)
                    nc.vector.scalar_tensor_tensor(out=out_, in0=src, scalar=scale, in1=hi,
                                                   op0=ALU.mult, op1=ALU.subtract).then_inc(done, 1)

                def shift(p):
                    if runs(HDS, s):
                        n = gs[HDS] * PAIRS + (p + 1)
                        sc = ps_s[:, :, 0:6 * NT].rearrange("p a (h k) -> p a h k", k=NT)
                        dve.wait_ge(p_s, n)
                        nc.vector.tensor_reduce(mx[:].rearrange("p (a h) -> p a h", a=2), sc, AX_X, ALU.max).then_inc(s_mx, 1)
                        dve.wait_ge(s_mx, n)
                        if p:
                            dve.wait_ge(s_p2, gs[HDS] * PAIRS + p)
                        nc.vector.tensor_tensor(df[:].rearrange("p (a h) k -> p a h k", a=2), sc,
                                                mx[:].rearrange("p (a h) -> p a h", a=2).unsqueeze(3).to_broadcast([128, 2, 6, NT]),
                                                ALU.subtract).then_inc(s_df, 1)

                def p2t(p):
                    if runs(HDS, s):
                        low(p2T[:, 1].rearrange("p (a b) c -> p a (b c)", a=2), ps_p[:, :, 0:3 * 128],
                            p2T[:, 0].rearrange("p (a b) c -> p a (b c)", a=2), 1.0, s_p2h, gs[HDS] * PAIRS + (p + 1), s_p2T)

                def norm2(p):
                    if runs(HDS, s):
                        dve.wait_ge(p_pv, gs[HDS] * PAIRS + (p + 1))
                        pv = bank(f"pv{p}")[:, 0:HEADS * 2 * (HD + 1)].rearrange("p (b h e) -> p b h e", b=2, e=HD + 1)
                        for b in range(2):
                            r = slice(SLOT * b, SLOT * (b + 1))
                            nc.vector.reciprocal(rc[r, :], pv[r, b, :, HD]).then_inc(s_rc, 1)
                        for b in range(2):
                            r = slice(SLOT * b, SLOT * (b + 1))
                            dve.wait_ge(s_rc, gs[HDS] * PAIRS * 2 + (2 * p + 1 + b))
                            nc.vector.tensor_tensor(o2[r, p, :].rearrange("p (h e) -> p h e", h=HEADS), pv[r, b, :, 0:HD],
                                                    rc[r, :].unsqueeze(2).to_broadcast([SLOT, HEADS, HD]),
                                                    ALU.mult).then_inc(s_o2, 1)

                def h_tile(t):
                    if runs(TOK, s):
                        g, m = gs[TOK], TILES[t][1]
                        n = g * 3 + (t + 1)
                        dve.wait_ge(p_tok, n)
                        if t == 0 and (not isinstance(s, int) or s > TOK):
                            dve.wait_ge(s_hp, g * 16 * HP_DMAS)
                        nc.vector.scalar_tensor_tensor(out=h[0:m, t, :], in0=ps_tok[0:m, 0:D], scalar=1 / WS,
                                                       in1=b_tok_bc[0:m, :], op0=ALU.mult, op1=ALU.add).then_inc(s_h, 1)
                        dve.wait_ge(s_h, n)
                        nc.vector.bn_stats(st1[0:m, t, :], h[0:m, t, :]).then_inc(s_ln1, 1)
                        dve.wait_ge(s_ln1, n)
                        nc.vector.memset(carrier[:], 0.0)
                        nc.vector.bn_aggr(mv1[0:m, t, :], st1[0:m, t, :]).then_inc(s_var1, 1)

                def xn_tile(t):
                    if runs(TOK, s):
                        g, m = gs[TOK], TILES[t][1]
                        dve.wait_ge(s_rs1, g * 3 + (t + 1))
                        nc.vector.tensor_scalar(xn[0:m, t, :], h[0:m, t, :], mv1[0:m, t, 0:1], rs1[0:m, t:t + 1],
                                                ALU.subtract, ALU.mult).then_inc(s_xn, 1)

                links = [0]

                def link(ins, last=False):
                    links[0] += 1
                    ins.then_inc(s_top, 1)
                    if not last:
                        dve.wait_ge(s_top, gs[MIX] * TOP_LINKS + links[0])

                def per_pair(ap):
                    return ap.unsqueeze(2).to_broadcast([PT_, PAIRS, N_EXP])

                def likeliest(k):
                    if runs(MIX, s):
                        src = (lg, lg2)[k]
                        if k == 0:
                            dve.wait_ge(s_ga, gs[MIX] * 2 + 2)
                            link(nc.vector.tensor_tensor(lg[:], ga[:, :, NR:NR + N_EXP],
                                                         b_gate_bc[:].unsqueeze(1).to_broadcast([PT_, PAIRS, N_EXP]), ALU.add))
                        link(nc.vector.tensor_reduce(top[:, k, :], src[:], AX_X, ALU.max))
                        if k == 0:
                            link(nc.vector.tensor_tensor(lgm[:], lg[:], per_pair(top[:, 0, :]), ALU.subtract))
                            assert links[0] == TOP_SHIFTED
                        link(nc.vector.tensor_tensor(key[:, k, :, :], src[:], per_pair(top[:, k, :]), ALU.is_equal))
                        link(nc.vector.tensor_tensor(hot[:, k, :, :], key[:, k, :, :], rank_row[:], ALU.mult))
                        link(nc.vector.tensor_reduce(best[:, k, :], hot[:, k, :, :], AX_X, ALU.max))
                        link(nc.vector.tensor_tensor(key[:, k, :, :], hot[:, k, :, :], per_pair(best[:, k, :]), ALU.is_equal))
                        if k == 0:
                            link(nc.vector.scalar_tensor_tensor(out=lg2[:], in0=key[:, 0, :, :], scalar=-3e38, in1=lg[:],
                                                                op0=ALU.mult, op1=ALU.add))

                def dispatch():
                    if runs(MIX, s):
                        link(nc.vector.tensor_tensor(both[:], key[:, 0, :, :], key[:, 1, :, :], ALU.add))
                        dve.wait_ge(s_pex, gs[MIX] + 1)
                        link(nc.vector.tensor_reduce(pe_s[:], pe_x[:], AX_X, ALU.add))
                        link(nc.vector.reciprocal(pe_r[:], pe_s[:]))
                        link(nc.vector.scalar_tensor_tensor(out=disp0[:], in0=both[:], scalar=LORA_SCALE, in1=pe_x[:],
                                                            op0=ALU.mult, op1=ALU.mult))
                        link(nc.vector.tensor_tensor(disp[:], disp0[:], per_pair(pe_r[:]), ALU.mult), last=True)
                        assert links[0] == TOP_LINKS

                def g_low(jh):
                    if runs(ATT, s):
                        low(gT[:, 1, jh, :], bank(f"g{jh}")[0:DH, 0:TG], gT[:, 0, jh, :], 1 / WS, s_gh, gs[ATT] * 2 + (jh + 1), s_gT)

                def max1():
                    if runs(ATT, s):
                        g = s - ATT
                        dve.wait_ge(p_sc, g + 1)
                        nc.vector.tensor_tensor(sm[:], bank("sc")[0:PT_, :].rearrange("p (a c) -> p a c", a=PAIRS)[:, :, 0:PT_],
                                                mask[:].unsqueeze(1).to_broadcast([PT_, PAIRS, PT_]), ALU.add).then_inc(s_sm, 1)
                        dve.wait_ge(s_sm, g + 1)
                        nc.vector.tensor_reduce(m1[:], sm[:], AX_X, ALU.max).then_inc(s_m1, 1)
                        dve.wait_ge(s_m1, g * 2 + 1)
                        nc.vector.tensor_scalar(nm1[:], m1[:], -1.0, None, ALU.mult).then_inc(s_m1, 1)

                def sum1():
                    if runs(ATT, s):
                        dve.wait_ge(s_p1, gs[ATT] * PAIRS + PAIRS)
                        nc.vector.reciprocal(rl1[:], l1[:]).then_inc(s_rl1, 1)

                def h2_(n):
                    if runs(ATT, s):
                        g, gp = gs[ATT], gpar[ATT]
                        if n == 0:
                            dve.wait_ge(s_rl1, g + 1)
                            dve.wait_ge(s_hp, (g + 1) * 16 * HP_DMAS)
                        dve.wait_ge(p_av, g * 2 + (n + 1))
                        for p in (2 * n, 2 * n + 1):
                            nc.vector.scalar_tensor_tensor(out=h2[:, gp, p, :],
                                                           in0=bank(f"av{n}")[0:PT_, D * (p % 2):D * (p % 2 + 1)],
                                                           scalar=rl1[:, p:p + 1], in1=hp[:, gp, p, :],
                                                           op0=ALU.mult, op1=ALU.add).then_inc(s_h2, 1)

                def stats2():
                    if runs(ATT, s):
                        g, gp = gs[ATT], gpar[ATT]
                        for p in range(PAIRS):
                            dve.wait_ge(s_h2, g * PAIRS + (p + 1))
                            nc.vector.bn_stats(st2[:, p, :], h2[:, gp, p, :]).then_inc(s_ln2, 1)
                        dve.wait_ge(s_ln2, g * 5 + PAIRS)
                        nc.vector.memset(carrier[:], 0.0)
                        for p in range(PAIRS):
                            ins = nc.vector.bn_aggr(mv2[:, p, :], st2[:, p, :])
                        ins.then_inc(s_ln2, 1)

                def xn2_():
                    if runs(ATT, s):
                        dve.wait_ge(s_rs2, gs[ATT] + 1)
                        for p in range(PAIRS):
                            nc.vector.tensor_scalar(xn2[:, p, :], h2[:, gpar[ATT], p, :], mv2[:, p, 0:1], rs2[:, p:p + 1],
                                                    ALU.subtract, ALU.mult).then_inc(s_xn2, 1)

                def ad_low():
                    if runs(MIX, s):
                        low(adT[:, 1, :], bank("at")[0:NR, 0:TG], adT[:, 0, :], 1.0, s_adh, gs[MIX] + 1, s_adT)

                def qk_low(t):
                    if runs(MIX, s):
                        dve.wait_ge(s_qkh, gs[MIX] * 3 + (t + 1))
                        nc.vector.scalar_tensor_tensor(out=qk[:, 1, t, :], in0=bank(f"qk{t}")[:, 0:TG], scalar=b_qk[:, t:t + 1],
                                                       in1=qk[:, 0, t, :], op0=ALU.add, op1=ALU.subtract).then_inc(s_qkl, 1)

                def cv_low(n):
                    if runs(MIX, s):
                        lo_, src = v2_split(n, 1)
                        low(lo_, src, v2_split(n, 0)[0], VS / WS, s_v2h, gs[MIX] * 2 + (n + 1), s_v2s)

                def o_low(kh):
                    if runs(HDS, s):
                        low(o2T[:, 1, kh, :].rearrange("p (a t) -> p a t", t=NT),
                            bank(f"ot{kh}")[0:DH, :].rearrange("p (a t) -> p a t", t=SLOT)[:, :, 0:NT],
                            o2T[:, 0, kh, :].rearrange("p (a t) -> p a t", t=NT), 1.0, s_oh, gs[HDS] * 2 + (kh + 1), s_o2T)

                def x2_low(kh):
                    if runs(ATT, s):
                        low(x2T[:, gpar[ATT], 1, kh, :], bank(f"x2t{kh}")[0:DH, 0:TG], x2T[:, gpar[ATT], 0, kh, :],
                            1.0, s_x2h, gs[ATT] * 2 + (kh + 1), s_x2T)

                def xn_low(kh):
                    if runs(TOK, s):
                        low(xnT[:, gpar[TOK], 1, kh, 0:TG], bank(f"xt{kh}")[0:DH, 0:TG], xnT[:, gpar[TOK], 0, kh, 0:TG],
                            1.0, s_xnh, gs[TOK] * 2 + (kh + 1), s_xnT)

                def fin(n):
                    if runs(HDS, s):
                        g, gp = gs[HDS], gpar[HDS]
                        if n == 0:
                            dve.wait_ge(s_h2b, g + 1)
                        dve.wait_ge(p_pr, g * 2 + (n + 1))
                        nc.vector.scalar_tensor_tensor(out=h2b[:, gp, 2 * n:2 * n + 2, :],
                                                       in0=bank(f"pr{n}")[0:PT_, 0:2 * D].rearrange("p (a c) -> p a c", a=2),
                                                       scalar=1 / (WS * VS), in1=h2b[:, gp, 2 * n:2 * n + 2, :],
                                                       op0=ALU.mult, op1=ALU.add).then_inc(s_fin, 1)

                shift(0)
                g_low(0)
                shift(1)
                likeliest(0)
                p2t(0)
                likeliest(1)
                g_low(1)
                dispatch()
                norm2(0)
                h_tile(0)
                max1()
                p2t(1)
                ad_low()
                norm2(1)
                shift(2)
                qk_low(0)
                cv_low(0)
                shift(3)
                qk_low(1)
                p2t(2)
                qk_low(2)
                h_tile(1)
                sum1()
                xn_tile(0)
                norm2(2)
                h2_(0)
                h2_(1)
                p2t(3)
                stats2()
                norm2(3)
                cv_low(1)
                xn2_()
                o_low(0)
                o_low(1)
                h_tile(2)
                x2_low(0)
                xn_tile(1)
                fin(0)
                xn_tile(2)
                fin(1)
                xn_low(0)
                x2_low(1)
                xn_low(1)

            program(dve, step)

        @block.tensor
        def _(pe):
            mm = nc.tensor.matmul

            def split_product(dst, stat, mov, start, stop):
                mm(dst, stat[0], mov[0], start=start, stop=False)
                mm(dst, stat[0], mov[1], start=False, stop=False)
                return mm(dst, stat[1], mov[0], start=False, stop=stop)

            pe.wait_ge(s_wt, 16)
            pe.wait_ge(s_ident, 1)
            for n, (parts, rows, cols, *_) in enumerate(UNITS):
                if n >= 3:
                    pe.wait_ge(s_ul, n - 2)
                if n == TOK_UNITS:
                    pe.wait_ge(s_w, 16 * N_LOADS)
                if n == M_FROM:
                    pe.wait_ge(s_ul, n)
                for kind, at, src in parts:
                    if kind == "t":
                        k, m = src.shape[0], src.shape[1]
                        last = nc.tensor.transpose(unit_bank(n, rows, cols)[:, at:at + k], src, ident[0:k, 0:k])
                    else:
                        for hh in range(2):
                            last = mm(unit_bank(n, rows, cols)[:, at:at + D], qk_T[:, D * hh + DH * src:D * hh + DH * src + DH],
                                      qk_T[:, 2 * D + D * hh:2 * D + D * hh + D], start=(hh == 0), stop=(hh == 1))
                last.then_inc(s_ut, 1)
            pe.wait_ge(s_ul, len(UNITS))
            pe.wait_ge(s_bv, 3)
            for kh in range(2):
                last = split_product(ps_s[0:PT_, 0, 0:D], [bias_v[:, part, kh, :] for part in range(2)],
                                     [w_pr[:, part, kh, :] for part in range(2)], kh == 0, kh == 1)
            last.then_inc(p_bv, 1)
            pe.wait_ge(s_wd, 2)
            pe.wait_ge(s_maskf, 16)

            def step(s, par):
                gs = {lag: s - lag for lag in range(5)}
                gpar = {lag: (par - lag) % 2 for lag in range(5)}

                def tok(k):
                    if not runs(TOK, s):
                        return
                    g, gp = gs[TOK], gpar[TOK]
                    t, q = k // 4, k % 4
                    t0, m = TILES[t]
                    if k == 0:
                        pe.wait_ge(s_lo, g * 16 + 16)
                        pe.wait_ge(s_xrow, g * 48 + 48)
                    if q == 0 and (not isinstance(s, int) or s > TOK or t > 0):
                        pe.wait_ge(s_h, g * 3 + t)
                    for j in range(3 * q, 3 * q + 3):
                        last = split_product(ps_tok[0:m, 0:D], [xs[:, gp, part, j, t0:t0 + m] for part in range(2)],
                                             [w_tok[:, part, j, :] for part in range(2)], j == 0, j == MAIN - 1)
                    if q == 3:
                        last.then_inc(p_tok, 1)

                def xt(kh):
                    if runs(TOK, s):
                        if kh == 0:
                            pe.wait_ge(s_xn, gs[TOK] * 3 + 3)
                        bank_free(pe, f"xt{kh}", s)
                        for t, (t0, m) in enumerate(TILES):
                            last = nc.tensor.transpose(bank(f"xt{kh}")[0:DH, t0:t0 + m],
                                                       xn[0:m, t, DH * kh:DH * (kh + 1)], ident[0:m, 0:m])
                        last.then_inc(p_xt, 1)

                def g_(jh):
                    if runs(ATT, s):
                        gp = gpar[ATT]
                        if jh == 0:
                            pe.wait_ge(s_xnT, gs[ATT] * 2 + 2)
                        bank_free(pe, f"g{jh}", s)
                        for kh in range(2):
                            last = split_product(bank(f"g{jh}")[0:DH, 0:TG],
                                                 [w_m[:, part, kh, DH * jh:DH * (jh + 1)] for part in range(2)],
                                                 [xnT[:, gp, part, kh, 0:TG] for part in range(2)], kh == 0, kh == 1)
                        last.then_inc(p_g, 1)

                def tokens_times(name, p, stat, mov, cols, first, stop=True):
                    dst = bank(name)[0:PT_, first:first + cols]
                    for kh in range(2):
                        last = split_product(dst, [stat(part, kh) for part in range(2)],
                                             [mov(part, kh) for part in range(2)], kh == 0, stop and kh == 1)
                    return last

                def v_(n):
                    if runs(ATT, s):
                        gp = gpar[ATT]
                        bank_free(pe, f"v{n}", s)
                        for p in (2 * n, 2 * n + 1):
                            last = tokens_times(f"v{n}", p, lambda part, kh: xnT[:, gp, part, kh, PT_ * p:PT_ * (p + 1)],
                                                lambda part, kh: w_v1[:, part, kh, :], D, D * (p % 2))
                        last.then_inc(p_v, 1)

                def sc():
                    if runs(ATT, s):
                        gp = gpar[ATT]
                        pe.wait_ge(s_gT, gs[ATT] * 2 + 2)
                        bank_free(pe, "sc", s)
                        for p in range(PAIRS):
                            last = tokens_times("sc", p, lambda part, kh: gT[:, part, kh, PT_ * p:PT_ * (p + 1)],
                                                lambda part, kh: xnT[:, gp, part, kh, PT_ * p:PT_ * p + 128], 128, 128 * p)
                        last.then_inc(p_sc, 1)

                def pt():
                    if runs(ATT, s):
                        pe.wait_ge(s_p1, gs[ATT] * PAIRS + PAIRS)
                        bank_free(pe, "pt", s)
                        for p in range(PAIRS):
                            last = nc.tensor.transpose(bank("pt")[0:PT_, PT_ * p:PT_ * (p + 1)], p1[:, p, :], ident[0:PT_, 0:PT_])
                        last.then_inc(p_pt, 1)

                def av(n):
                    if runs(ATT, s):
                        if n == 0:
                            pe.wait_ge(s_p1T, gs[ATT] + 1)
                            pe.wait_ge(s_v1, gs[ATT] * 2 + 2)
                        bank_free(pe, f"av{n}", s)
                        for p in (2 * n, 2 * n + 1):
                            last = mm(bank(f"av{n}")[0:PT_, D * (p % 2):D * (p % 2 + 1)], p1T[:, p, :], v1[:, p, :],
                                      start=True, stop=True)
                        last.then_inc(p_av, 1)

                def x2t(kh):
                    if runs(ATT, s):
                        if kh == 0:
                            pe.wait_ge(s_xn2, gs[ATT] * PAIRS + PAIRS)
                        bank_free(pe, f"x2t{kh}", s)
                        for p in range(PAIRS):
                            last = nc.tensor.transpose(bank(f"x2t{kh}")[0:DH, PT_ * p:PT_ * (p + 1)],
                                                       xn2[:, p, DH * kh:DH * (kh + 1)], ident[0:PT_, 0:PT_])
                        last.then_inc(p_x2t, 1)

                def ga_(n):
                    if runs(MIX, s):
                        gp = gpar[MIX]
                        if n == 0:
                            pe.wait_ge(s_x2T, gs[MIX] * 2 + 2)
                        bank_free(pe, f"ga{n}", s)
                        for p in (2 * n, 2 * n + 1):
                            last = tokens_times(f"ga{n}", p, lambda part, kh: x2T[:, gp, part, kh, PT_ * p:PT_ * (p + 1)],
                                                lambda part, kh: w_ga[:, part, kh, :], NR + N_EXP, (NR + N_EXP) * (p % 2))
                        last.then_inc(p_ga, 1)

                def at():
                    if runs(MIX, s):
                        pe.wait_ge(s_ad, gs[MIX] + 1)
                        bank_free(pe, "at", s)
                        for p in range(PAIRS):
                            last = nc.tensor.transpose(bank("at")[0:NR, PT_ * p:PT_ * (p + 1)], ad[:, p, :], ident[0:PT_, 0:PT_])
                        last.then_inc(p_at, 1)

                def qk_(t):
                    if runs(MIX, s):
                        gp = gpar[MIX]
                        if t == 0:
                            pe.wait_ge(s_adT, gs[MIX] + 1)
                        bank_free(pe, f"qk{t}", s)
                        dst = bank(f"qk{t}")[:, 0:TG]
                        cols = slice(128 * t, 128 * (t + 1))
                        for kh in range(2):
                            split_product(dst, [w_qk[:, part, kh, cols] for part in range(2)],
                                          [x2T[:, gp, part, kh, :] for part in range(2)], kh == 0, False)
                        split_product(dst, [w_lora[:, part, cols] for part in range(2)],
                                      [adT[:, part, :] for part in range(2)], False, True).then_inc(p_qk, 1)

                def cv(n):
                    if runs(MIX, s):
                        gp = gpar[MIX]
                        bank_free(pe, f"cv{n}", s)
                        by_half = bank(f"cv{n}")[0:PT_, 0:2 * D].rearrange("p (s a c) -> p a s c", s=2, a=2)
                        for p in (2 * n, 2 * n + 1):
                            tok_p = slice(PT_ * p, PT_ * (p + 1))
                            for kh in range(2):
                                split_product(by_half[:, p % 2], [x2T[:, gp, part, kh, tok_p] for part in range(2)],
                                              [w_v2[:, part, kh, :] for part in range(2)], kh == 0, False)
                            last = split_product(by_half[:, p % 2],
                                                 [adT[:, part, tok_p] for part in range(2)],
                                                 [w_lora[:, part, 2 * D:3 * D] for part in range(2)], False, True)
                        last.then_inc(p_cv, 1)

                def s_(p):
                    if runs(HDS, s):
                        g = gs[HDS]
                        if p == 0:
                            pe.wait_ge(s_qk3, (g + 1) * 96)
                        if p or not isinstance(s, int) or s > HDS:
                            pe.wait_ge(s_df, g * PAIRS + p)
                        for hh in range(HEADS):
                            for b in range(2):
                                m = 128 if hh + b == 0 else SLOT
                                t0 = PT_ * p + NT * b
                                last = mm(ps_s[SLOT * b:SLOT * b + m, hh // 6, NT * (hh % 6):NT * (hh % 6 + 1)],
                                          q3[0:3 * HD, hh, t0:t0 + m], k3[0:3 * HD, hh, t0:t0 + NT], start=True, stop=True)
                        last.then_inc(p_s, 1)

                def p_(p):
                    if runs(HDS, s):
                        g = gs[HDS]
                        pe.wait_ge(s_p2, g * PAIRS + (p + 1))
                        if p or not isinstance(s, int) or s > HDS:
                            pe.wait_ge(s_p2T, g * PAIRS + p)
                        for half in range(2):
                            for a in range(3):
                                last = nc.tensor.transpose(ps_p[:, half, 128 * a:128 * (a + 1)],
                                                           p2[:, 6 * half + 2 * a:6 * half + 2 * a + 2, :].rearrange("p a b -> p (a b)"),
                                                           ident[:])
                        last.then_inc(p_p, 1)

                def pv(p):
                    if runs(HDS, s):
                        g, gp = gs[HDS], gpar[HDS]
                        if p == 0:
                            pe.wait_ge(s_v2, (g + 1) * 64)
                        pe.wait_ge(s_p2T, g * PAIRS + (p + 1))
                        bank_free(pe, f"pv{p}", s)
                        dst = bank(f"pv{p}")[:, 0:2 * HEADS * (HD + 1)].rearrange("p (b h e) -> p b h e", b=2, e=HD + 1)
                        for j in range(HEADS // 2):
                            last = split_product(dst[:, :, 2 * j:2 * j + 2, :],
                                                 [p2T[:, part, j, :] for part in range(2)],
                                                 [v2[:, gp, :, :, part, p, j, :] for part in range(2)], True, True)
                        last.then_inc(p_pv, 1)

                def ot(kh):
                    if runs(HDS, s):
                        if kh == 0:
                            pe.wait_ge(s_o2, gs[HDS] * 8 + 8)
                        bank_free(pe, f"ot{kh}", s)
                        for p in range(PAIRS):
                            last = nc.tensor.transpose(bank(f"ot{kh}")[0:DH, 128 * p:128 * (p + 1)],
                                                       o2[:, p, DH * kh:DH * (kh + 1)], ident[:])
                        last.then_inc(p_ot, 1)

                def pr(n):
                    if runs(HDS, s):
                        if n == 0:
                            pe.wait_ge(s_o2T, gs[HDS] * 2 + 2)
                        bank_free(pe, f"pr{n}", s)
                        for p in (2 * n, 2 * n + 1):
                            last = tokens_times(f"pr{n}", p, lambda part, kh: o2T[:, part, kh, PT_ * p:PT_ * (p + 1)],
                                                lambda part, kh: w_pr[:, part, kh, :], D, D * (p % 2))
                        last.then_inc(p_pr, 1)

                s_(0)
                tok(0)
                tok(1)
                g_(0)
                ga_(0)
                s_(1)
                ga_(1)
                p_(0)
                g_(1)
                tok(2)
                v_(0)
                tok(3)
                pv(0)
                p_(1)
                sc()
                s_(2)
                v_(1)
                at()
                tok(4)
                tok(5)
                pv(1)
                qk_(0)
                cv(0)
                s_(3)
                qk_(1)
                p_(2)
                qk_(2)
                tok(6)
                tok(7)
                pt()
                pv(2)
                av(0)
                p_(3)
                av(1)
                tok(8)
                cv(1)
                pv(3)
                tok(9)
                tok(10)
                ot(0)
                ot(1)
                tok(11)
                x2t(0)
                pr(0)
                pr(1)
                x2t(1)
                xt(0)
                xt(1)

            program(pe, step)


def f32_of(ap):
    names = ["a", "b", "c", "d"][:len(ap.shape) - 1]
    return ap.rearrange(f"p {' '.join(names)} -> p ({' '.join(names)})").bitcast(F32)


def as_shape(src, like, odd=None):
    if odd is not None:
        return src.rearrange("p (h s e) -> p s h e", s=2, e=HD)[:, odd]
    if len(like.shape) == 2:
        return src
    return src.rearrange("p (a c) -> p a c", a=like.shape[1])


_INS = ["x", "L0_tok_W", "L0_tok_b", "L0_attn_Wq", "L0_attn_Wk", "L0_attn_Wv", "L0_ffn_W_qkv", "L0_ffn_b_qkv",
        "L0_ffn_W_gate", "L0_ffn_b_gate", "L0_ffn_A", "L0_ffn_B_lora", "L0_ffn_W_proj", "L0_ffn_b_proj"]


def kernel(**inputs):
    import numpy as np
    import concourse.bacc as bacc
    from concourse.bass_utils import run_bass_kernel_spmd

    nc = bacc.Bacc("TRN2", target_bir_lowering=False, num_devices=1)
    arrays, args = {}, []
    for name in _INS:
        a = np.ascontiguousarray(inputs[name])
        arrays[name] = a
        args.append(nc.dram_tensor(name, a.shape, mybir.dt.from_np(a.dtype), kind="ExternalInput").ap())
    out = nc.dram_tensor("out", (B, NT, D), F32, kind="ExternalOutput").ap()
    scratch = nc.dram_tensor("qk_scratch", (2, 2, 2 * D, TG), F16, kind="Internal").ap()
    audio_tower(nc, *args, out, scratch)
    r = run_bass_kernel_spmd(nc, [arrays], core_ids=[0])
    return r.results[0]["out"]
```
